# Optimizing a Trainium2 kernel written in Bass

```python
import numpy as np
import jax
import jax.numpy as jnp

def _softmax(x, axis=-1):
    return jax.nn.softmax(x, axis=axis)

def _gelu(x):
    return jax.nn.gelu(x, approximate=True)

def _silu(x):
    return jax.nn.silu(x)

def _sigmoid(x):
    return jax.nn.sigmoid(x)

def _layernorm(x, axis=-1, eps=1e-05):
    m = jnp.mean(x, axis=axis, keepdims=True)
    v = jnp.var(x, axis=axis, keepdims=True)
    return (x - m) / jnp.sqrt(v + eps)

def _scatter_add(tgt, idx, src, axis=0):
    return tgt.at[idx].add(src)

def _segment_sum(src, seg, n):
    return jax.ops.segment_sum(src, seg, n)
kernel_name = 'mk_xattn_seq_d1_seqx_r2_56a0f2'

def setup_inputs(seed: int=0):
    np.random.seed(seed)
    _w = jnp.asarray

    def _rec_inputs():
        import jax
        import jax.numpy as jnp
        _rk = jax.random.key(seed)
        x = -0.0002928 + 1 * jax.random.normal(jax.random.fold_in(_rk, 1), (16, 256, 512), jnp.float32)
        _lenS = 256 - jax.random.randint(jax.random.fold_in(_rk, 7), (16,), 0, max(1, 256 // 4) + 1, jnp.int32)
        _lenS2 = 256 - jax.random.randint(jax.random.fold_in(_rk, 8), (16,), 0, max(1, 256 // 4) + 1, jnp.int32)
        _ctx_1024P = jax.random.normal(jax.random.fold_in(_rk, 11), (16, 16, 512), jnp.float32)
        _ctx_1024c = jax.random.dirichlet(jax.random.fold_in(_rk, 511), 0.3 * jnp.ones((16,), jnp.float32), (16, 256))
        _ctx_1024t = jnp.einsum('bsk,bkd->bsd', _ctx_1024c, _ctx_1024P)
        _ctx_1024t = _ctx_1024t * jax.lax.rsqrt(jnp.mean(jnp.square(_ctx_1024t)) + 1e-12) * 0.953939
        ctx_1024 = -1.39393e-06 + 0.999914 * (_ctx_1024t + 0.3 * jax.random.normal(jax.random.fold_in(_rk, 611), (16, 256, 512), jnp.float32))
        return (x, ctx_1024)
    x, ctx_1024 = _rec_inputs()

    def _L0_xattn_setup():
        import jax, jax.numpy as jnp
        import numpy as np
        NEG = -1e+32
        EPS_LN = 1e-05

        def _layer_norm(x, w, b):
            mu = jnp.mean(x, axis=-1, keepdims=True)
            var = jnp.mean((x - mu) ** 2, axis=-1, keepdims=True)
            return (x - mu) / jnp.sqrt(var + EPS_LN) * w + b

        def _forward(query, key, values, Wk, bk, Wv, bv, Wo, bo, gammas, ln1_w, ln1_b, W1, b1, W2, b2, ln2_w, ln2_b, mask):
            B, S, D = query.shape
            H = gammas.shape[0]
            dk = D // H

            def proj(x, W, b):
                return (x @ W.T + b).reshape(B, S, H, dk).transpose(0, 2, 1, 3)
            q = proj(query, Wk, bk)
            k = proj(key, Wk, bk)
            v = proj(values, Wv, bv)
            scores = jnp.einsum('bhqd,bhkd->bhqk', q, k) / np.sqrt(dk).astype(np.float32)
            allow = jnp.tril(jnp.ones((S, S), bool), k=mask - 1)[None, None]
            scores_ = jax.nn.softmax(jnp.where(allow, scores, NEG), axis=-1)
            scores_ = scores_ * allow.astype(scores_.dtype)
            distcum = jnp.cumsum(scores_, axis=-1)
            disttotal = jnp.sum(scores_, axis=-1, keepdims=True)
            idx = jnp.arange(S)
            position_effect = jnp.abs(idx[:, None] - idx[None, :]).astype(jnp.float32)[None, None]
            dist_scores = jnp.sqrt(jnp.clip((disttotal - distcum) * position_effect, 0.0, None))
            gamma = -jax.nn.softplus(gammas)[None]
            total_effect = jnp.clip(jnp.exp(dist_scores * gamma), 1e-05, 100000.0)
            total_effect = jax.lax.stop_gradient(total_effect)
            scores = scores * total_effect
            scores = jnp.where(allow, scores, NEG)
            attn = jax.nn.softmax(scores, axis=-1)
            out = jnp.einsum('bhqk,bhkd->bhqd', attn, v)
            concat = out.transpose(0, 2, 1, 3).reshape(B, S, D)
            query2 = concat @ Wo.T + bo
            x = _layer_norm(query + query2, ln1_w, ln1_b)
            ff = jax.nn.relu(x @ W1.T + b1) @ W2.T + b2
            x = _layer_norm(x + ff, ln2_w, ln2_b)
            return x
        key = jax.random.key(seed)
        ks = jax.random.split(key, 10)
        B, S, D, H, F = (2, 1024, 512, 16, 2048)
        s = 0.02
        return {'query': jax.random.normal(ks[0], (B, S, D), jnp.float32), 'key': jax.random.normal(ks[1], (B, S, D), jnp.float32), 'values': jax.random.normal(ks[2], (B, S, D), jnp.float32), 'Wk': jax.random.normal(ks[3], (D, D), jnp.float32) * s, 'bk': jnp.zeros((D,), jnp.float32), 'Wv': jax.random.normal(ks[4], (D, D), jnp.float32) * s, 'bv': jnp.zeros((D,), jnp.float32), 'Wo': jax.random.normal(ks[5], (D, D), jnp.float32) * s, 'bo': jnp.zeros((D,), jnp.float32), 'gammas': jax.random.normal(ks[6], (H, 1, 1), jnp.float32), 'ln1_w': jnp.ones((D,), jnp.float32), 'ln1_b': jnp.zeros((D,), jnp.float32), 'W1': jax.random.normal(ks[7], (F, D), jnp.float32) * s, 'b1': jnp.zeros((F,), jnp.float32), 'W2': jax.random.normal(ks[8], (D, F), jnp.float32) * s, 'b2': jnp.zeros((D,), jnp.float32), 'ln2_w': jnp.ones((D,), jnp.float32), 'ln2_b': jnp.zeros((D,), jnp.float32), 'mask': 1}
    _L0_xattn_all = _L0_xattn_setup()
    _L0_xattn_in = {k: v for k, v in _L0_xattn_all.items() if k in ('Wk', 'bk', 'Wv', 'bv', 'Wo', 'bo', 'gammas', 'ln1_w', 'ln1_b', 'W1', 'b1', 'W2', 'b2', 'ln2_w', 'ln2_b')}
    del _L0_xattn_all
    return {'x': x, 'ctx_1024': ctx_1024, 'L0_xattn_Wk': _L0_xattn_in['Wk'], 'L0_xattn_bk': _L0_xattn_in['bk'], 'L0_xattn_Wv': _L0_xattn_in['Wv'], 'L0_xattn_bv': _L0_xattn_in['bv'], 'L0_xattn_Wo': _L0_xattn_in['Wo'], 'L0_xattn_bo': _L0_xattn_in['bo'], 'L0_xattn_gammas': _L0_xattn_in['gammas'], 'L0_xattn_ln1_w': _L0_xattn_in['ln1_w'], 'L0_xattn_ln1_b': _L0_xattn_in['ln1_b'], 'L0_xattn_W1': _L0_xattn_in['W1'], 'L0_xattn_b1': _L0_xattn_in['b1'], 'L0_xattn_W2': _L0_xattn_in['W2'], 'L0_xattn_b2': _L0_xattn_in['b2'], 'L0_xattn_ln2_w': _L0_xattn_in['ln2_w'], 'L0_xattn_ln2_b': _L0_xattn_in['ln2_b']}

def reference(x, ctx_1024, L0_xattn_Wk, L0_xattn_bk, L0_xattn_Wv, L0_xattn_bv, L0_xattn_Wo, L0_xattn_bo, L0_xattn_gammas, L0_xattn_ln1_w, L0_xattn_ln1_b, L0_xattn_W1, L0_xattn_b1, L0_xattn_W2, L0_xattn_b2, L0_xattn_ln2_w, L0_xattn_ln2_b):
    import jax
    import jax.numpy as jnp

    def _L0_xattn_ref(query, key, values, Wk, bk, Wv, bv, Wo, bo, gammas, ln1_w, ln1_b, W1, b1, W2, b2, ln2_w, ln2_b, mask):
        import jax, jax.numpy as jnp
        import numpy as np
        NEG = -1e+32
        EPS_LN = 1e-05

        def _layer_norm(x, w, b):
            mu = jnp.mean(x, axis=-1, keepdims=True)
            var = jnp.mean((x - mu) ** 2, axis=-1, keepdims=True)
            return (x - mu) / jnp.sqrt(var + EPS_LN) * w + b

        def _forward(query, key, values, Wk, bk, Wv, bv, Wo, bo, gammas, ln1_w, ln1_b, W1, b1, W2, b2, ln2_w, ln2_b, mask):
            B, S, D = query.shape
            H = gammas.shape[0]
            dk = D // H

            def proj(x, W, b):
                return (x @ W.T + b).reshape(B, S, H, dk).transpose(0, 2, 1, 3)
            q = proj(query, Wk, bk)
            k = proj(key, Wk, bk)
            v = proj(values, Wv, bv)
            scores = jnp.einsum('bhqd,bhkd->bhqk', q, k) / np.sqrt(dk).astype(np.float32)
            allow = jnp.tril(jnp.ones((S, S), bool), k=mask - 1)[None, None]
            scores_ = jax.nn.softmax(jnp.where(allow, scores, NEG), axis=-1)
            scores_ = scores_ * allow.astype(scores_.dtype)
            distcum = jnp.cumsum(scores_, axis=-1)
            disttotal = jnp.sum(scores_, axis=-1, keepdims=True)
            idx = jnp.arange(S)
            position_effect = jnp.abs(idx[:, None] - idx[None, :]).astype(jnp.float32)[None, None]
            dist_scores = jnp.sqrt(jnp.clip((disttotal - distcum) * position_effect, 0.0, None))
            gamma = -jax.nn.softplus(gammas)[None]
            total_effect = jnp.clip(jnp.exp(dist_scores * gamma), 1e-05, 100000.0)
            total_effect = jax.lax.stop_gradient(total_effect)
            scores = scores * total_effect
            scores = jnp.where(allow, scores, NEG)
            attn = jax.nn.softmax(scores, axis=-1)
            out = jnp.einsum('bhqk,bhkd->bhqd', attn, v)
            concat = out.transpose(0, 2, 1, 3).reshape(B, S, D)
            query2 = concat @ Wo.T + bo
            x = _layer_norm(query + query2, ln1_w, ln1_b)
            ff = jax.nn.relu(x @ W1.T + b1) @ W2.T + b2
            x = _layer_norm(x + ff, ln2_w, ln2_b)
            return x
        return _forward(query, key, values, Wk, bk, Wv, bv, Wo, bo, gammas, ln1_w, ln1_b, W1, b1, W2, b2, ln2_w, ln2_b, mask)
    x = _L0_xattn_ref(x, ctx_1024, ctx_1024, L0_xattn_Wk, L0_xattn_bk, L0_xattn_Wv, L0_xattn_bv, L0_xattn_Wo, L0_xattn_bo, L0_xattn_gammas, L0_xattn_ln1_w, L0_xattn_ln1_b, L0_xattn_W1, L0_xattn_b1, L0_xattn_W2, L0_xattn_b2, L0_xattn_ln2_w, L0_xattn_ln2_b, 1)
    return x

_drawn_inputs = setup_inputs


def setup_inputs(seed=0):
    import zlib

    import numpy as np

    out = dict(_drawn_inputs(seed))
    spreads = {'L0_xattn_bk': (0.0, 0.8),
     'L0_xattn_bv': (0.0, 0.1),
     'L0_xattn_bo': (0.0, 0.1),
     'L0_xattn_ln1_w': (1.0, 0.2),
     'L0_xattn_ln1_b': (0.0, 0.1),
     'L0_xattn_b1': (0.0, 0.1),
     'L0_xattn_b2': (0.0, 0.1),
     'L0_xattn_ln2_w': (1.0, 0.2),
     'L0_xattn_ln2_b': (0.0, 0.1)}
    factors = {'L0_xattn_Wk': 8.0, 'L0_xattn_gammas': 8.0}
    for name, (base, spread) in spreads.items():
        noise = np.random.default_rng([zlib.crc32(name.encode()), seed]).standard_normal(out[name].shape)
        drawn = base * np.exp(spread * noise) if base else spread * noise
        out[name] = jnp.asarray(drawn.astype(out[name].dtype))
    for name, factor in factors.items():
        out[name] = (out[name] * factor).astype(out[name].dtype)
    return out
```

```python
from contextlib import ExitStack

import concourse.bass as bass
from concourse import mybir

F32 = mybir.dt.float32
F32R = mybir.dt.float32r
I32 = mybir.dt.int32
ALU = mybir.AluOpType
ACT = mybir.ActivationFunctionType
AX_X = mybir.AxisListType.X

P = 128
NEG = -1e32
EPS_LN = 1e-5
R_MAX = 132.54745276195996
R_TINY = 1e-30


def build(nc, x_rows, x_t, ctx_t, wk, bk, wv, bv, wo, bo, gammas, ln1_w, ln1_b,
          w1, b1, w2, b2, ln2_w, ln2_b, out):
    B, S, D = x_rows.shape
    H = gammas.shape[0]
    F = b1.shape[1] * P
    DK = D // H
    KT = D // P
    RT = S // P
    NQ = D // P
    HQ = P // DK
    FT = F // P
    SCALE = 1.0 / float(DK) ** 0.5
    assert RT == 2 and HQ == 4 and NQ == 4
    LATE, EARLY = S, P
    SPAN = LATE + EARLY
    BLK = SPAN + 2
    QW = HQ * BLK
    GR = 512
    GT = GR // P
    NG = B * S // GR

    x1_dram = nc.dram_tensor("x1_rows", (B * S, D), F32, kind="Internal").ap()
    x1_by_batch = x1_dram.rearrange("(b t p) n -> b p t n", b=B, p=P)
    x1_by_group = x1_dram.rearrange("(g t p) n -> g p t n", g=NG, p=P)
    x_by_batch = x_rows.rearrange("b (t p) n -> b p t n", p=P)
    out_by_group = out.rearrange("b s n -> (b s) n").rearrange("(g t p) n -> g p t n", g=NG, p=P)

    with ExitStack() as whole:
        def sem(name):
            return whole.enter_context(nc.semaphore(name))

        def tensor(stack, name, shape, dt=F32):
            return stack.enter_context(nc.sbuf_tensor(name, shape, dt))

        bank = [whole.enter_context(nc.psum_tensor(f"bank{i}", [P, 512], F32)) for i in range(8)]

        ident = tensor(whole, "ident", [P, P])
        half = tensor(whole, "minus_half", [P, GT])
        tiny = tensor(whole, "tiny", [P, 1])

        ph1 = ExitStack()
        wk_hi, wk_lo, wv_hi, wv_lo, wo_hi, wo_lo = (
            tensor(ph1, n, [P, KT, D], F32R) for n in ("wk_hi", "wk_lo", "wv_hi", "wv_lo", "wo_hi", "wo_lo"))
        x_raw = tensor(ph1, "x_raw", [P, KT, S])
        c_raw = tensor(ph1, "c_raw", [P, KT, S])
        x_hi, x_lo, c_hi, c_lo = (tensor(ph1, n, [P, KT, S], F32R) for n in ("x_hi", "x_lo", "c_hi", "c_lo"))
        qk_parts = tensor(ph1, "qk_parts", [P, 4, S], F32R)
        stack = tensor(ph1, "stack", [P, 2, HQ, 2, S], F32R)
        v_sb = tensor(ph1, "v_sb", [P, 2, RT, D])
        s_sb = tensor(ph1, "s_sb", [P, NQ, HQ, SPAN])
        w_sb = tensor(ph1, "w_sb", [P, NQ, QW])
        p_sb = tensor(ph1, "p_sb", [P, HQ, SPAN])
        pt_sb = tensor(ph1, "pt_sb", [P, 2, HQ, SPAN])
        zr_sb = tensor(ph1, "zr_sb", [P, S])
        cc_sb = tensor(ph1, "cc_sb", [P, 2, S])
        cc_hi = tensor(ph1, "cc_hi", [P, NQ, S], F32R)
        cc_lo = tensor(ph1, "cc_lo", [P, NQ, S], F32R)
        xrow = tensor(ph1, "xrow", [P, RT, D])
        u_sb = tensor(ph1, "u_sb", [P, RT, D])
        bv_bc, bo_bc, l1w_bc, l1b_bc = (tensor(ph1, n, [P, D]) for n in ("bv_bc", "bo_bc", "l1w_bc", "l1b_bc"))
        bk_col = tensor(ph1, "bk_col", [P, NQ])
        iota_i = tensor(ph1, "iota_i", [P, S], I32)
        dist = tensor(ph1, "dist", [P, S])
        mask = tensor(ph1, "mask", [P, S])
        carry = tensor(ph1, "carry", [P, QW])
        ones = tensor(ph1, "ones", [P, DK])
        g_in = tensor(ph1, "g_in", [P, H])
        g_tmp = tensor(ph1, "g_tmp", [P, 8, H])
        gamma2 = tensor(ph1, "gamma2", [P, H, 2])
        m1, nm1, zi, gz, m2, nm2 = (tensor(ph1, n, [P, NQ, HQ, 2]) for n in ("m1", "nm1", "zi", "gz", "m2", "nm2"))
        bn1 = tensor(ph1, "bn1", [P, RT, 6])
        mv1 = tensor(ph1, "mv1", [P, RT, 2])
        rstd1 = tensor(ph1, "rstd1", [P, RT])
        ph1.close()

        w1_hi, w1_lo = (tensor(whole, n, [P, FT, KT, P], F32R) for n in ("w1_hi", "w1_lo"))
        w2_hi, w2_lo = (tensor(whole, n, [P, FT, D], F32R) for n in ("w2_hi", "w2_lo"))
        w_raw = tensor(whole, "w_raw", [P, 2, 2, 512])
        x1 = tensor(whole, "x1", [P, 2, GT, D])
        xt_hi, xt_lo = (tensor(whole, n, [P, KT, GR], F32R) for n in ("xt_hi", "xt_lo"))
        h_sb = tensor(whole, "h_sb", [P, 2, GR])
        h_hi, h_lo = (tensor(whole, n, [P, 2, GR], F32R) for n in ("h_hi", "h_lo"))
        y_sb = tensor(whole, "y_sb", [P, GT, D])
        b2_bc, l2w_bc, l2b_bc = (tensor(whole, n, [P, D]) for n in ("b2_bc", "l2w_bc", "l2b_bc"))
        b1_col = tensor(whole, "b1_col", [P, FT])
        bn2 = tensor(whole, "bn2", [P, GT, 6])
        mv2 = tensor(whole, "mv2", [P, GT, 2])
        rstd2 = tensor(whole, "rstd2", [P, GT])

        wraw_in = sem("wraw_in")
        cons_in = sem("cons_in")
        const_ok = sem("const_ok")
        w_hi_ok = sem("w_hi_ok")
        w_lo_ok = sem("w_lo_ok")
        gam_act = sem("gam_act")
        gam_dve = sem("gam_dve")
        xraw_in = sem("xraw_in")
        craw_in = sem("craw_in")
        xrow_in = sem("xrow_in")
        xc_hi_ok = sem("xc_hi_ok")
        xc_lo_ok = sem("xc_lo_ok")
        qk_mm = sem("qk_mm")
        v_mm = sem("v_mm")
        wo_mm = sem("wo_mm")
        qk_hi_ok = sem("qk_hi_ok")
        qk_lo_ok = sem("qk_lo_ok")
        stack_in = [sem(f"stack_in{n}") for n in range(2)]
        v_ok = sem("v_ok")
        s_mm = sem("s_mm")
        s_ok = sem("s_ok")
        nm1_ok = sem("nm1_ok")
        e1_ok = sem("e1_ok")
        zero_ok = sem("zero_ok")
        scan_ok = sem("scan_ok")
        zi_ok = sem("zi_ok")
        gz_ok = sem("gz_ok")
        t_ok = sem("t_ok")
        r_ok = sem("r_ok")
        root_ok = sem("root_ok")
        te_ok = sem("te_ok")
        s2_ok = sem("s2_ok")
        nm2_ok = sem("nm2_ok")
        p_ok = sem("p_ok")
        pt_mm = sem("pt_mm")
        pt_ok = sem("pt_ok")
        av_mm = sem("av_mm")
        zr_ok = sem("zr_ok")
        cc_ok = sem("cc_ok")
        cc_hi_ok = sem("cc_hi_ok")
        cc_lo_ok = sem("cc_lo_ok")
        xb_ok = sem("xb_ok")
        u_ok = sem("u_ok")
        bn1_ok = sem("bn1_ok")
        mv1_ok = sem("mv1_ok")
        ve1_ok = sem("ve1_ok")
        rstd1_ok = sem("rstd1_ok")
        norm1_ok = sem("norm1_ok")
        scaled1_ok = sem("scaled1_ok")
        x1_ok = sem("x1_ok")
        x1_out = sem("x1_out")

        ffw_in = [sem(f"ffw_in{n}") for n in range(2)]
        ffw_hi_ok = sem("ffw_hi_ok")
        ffw_lo_ok = sem("ffw_lo_ok")
        ffc_in = sem("ffc_in")
        x1_in = [sem(f"x1_in{n}") for n in range(2)]
        xt_mm = sem("xt_mm")
        xt_hi_ok = sem("xt_hi_ok")
        xt_lo_ok = sem("xt_lo_ok")
        h_mm = sem("h_mm")
        h_ok = sem("h_ok")
        h_hi_ok = sem("h_hi_ok")
        h_lo_ok = sem("h_lo_ok")
        y_step = sem("y_step")
        xb2_ok = sem("xb2_ok")
        y_ok = sem("y_ok")
        bn2_ok = sem("bn2_ok")
        mv2_ok = sem("mv2_ok")
        ve2_ok = sem("ve2_ok")
        rstd2_ok = sem("rstd2_ok")
        norm2_ok = sem("norm2_ok")
        scaled2_ok = sem("scaled2_ok")
        out_ok = sem("out_ok")
        out_st = sem("out_st")

        s_bank, pt_bank, av_bank, pj_bank = bank[0:2], bank[2:4], bank[4:6], bank[6:8]
        y_bank, h_bank, xt_bank = bank[0:4], bank[4:6], bank[6:8]

        def head_block(c, h, late):
            at = h * BLK + (0 if late else LATE + 1)
            return at, at + (LATE if late else EARLY)

        def three_passes(pe, dst, a_hi, a_lo, b_hi, b_lo, start, stop):
            nc.tensor.matmul(dst, a_hi, b_hi, start=start, stop=False)
            nc.tensor.matmul(dst, a_hi, b_lo, start=False, stop=False)
            return nc.tensor.matmul(dst, a_lo, b_hi, start=False, stop=stop)

        def over_batches(engine, step):
            step(0, True, False, False)
            step(1, True, True, False)
            with engine.Fori(1, B // 2) as j:
                step(j * 2, True, True, True)
                step(j * 2 + 1, True, True, True)
            step(B, False, True, True)
            step(B + 1, False, False, True)

        def over_groups(engine, group):
            group(0, 0, True, False)
            with engine.Fori(1, NG // 2) as j:
                group(j * 2 - 1, 1, False, False)
                group(j * 2, 0, False, False)
            group(NG - 1, 1, False, True)

        carried = sem("carried")

        def alone(engine):
            engine.sem_inc(carried)

        block = whole.enter_context(nc.Block())

        @block.sync
        def _(sp):
            for n, w in enumerate((wk, wv, wo)):
                sp.dma_start(s_sb_flat(s_sb)[:, n * KT * D:(n + 1) * KT * D],
                             w.rearrange("p k n -> p (k n)")).then_inc(wraw_in, 16)
            sp.dma_start(x_raw[:], x_t[0]).then_inc(xraw_in, 16)
            sp.dma_start(c_raw[:], ctx_t[0]).then_inc(craw_in, 16)
            for dst, src in ((bv_bc, bv), (bo_bc, bo), (l1w_bc, ln1_w), (l1b_bc, ln1_b), (g_in, gammas)):
                sp.dma_start(dst[:], src.partition_broadcast(P)).then_inc(cons_in, 16)
            sp.dma_start(bk_col[:], bk).then_inc(cons_in, 16)
            sp.dma_start(xrow[:], x_by_batch[0]).then_inc(xrow_in, 16)

            def next_inputs(i):
                sp.wait_ge(xc_lo_ok, 2 * i + 2)
                alone(sp)
                sp.dma_start(x_raw[:], x_t[i + 1]).then_inc(xraw_in, 16)
                sp.dma_start(c_raw[:], ctx_t[i + 1]).then_inc(craw_in, 16)

            def step(i, scores, attend, project, more=True):
                for c in range(NQ):
                    if not scores:
                        break
                    sp.wait_ge(qk_lo_ok, NQ * i + c + 1)
                    alone(sp)
                    if c >= 2:
                        sp.wait_ge(s_mm, 16 * i + 4 * (c - 1))
                    elif attend:
                        sp.wait_ge(s_mm, 16 * i + 4 * (c - 1))
                    for h in range(HQ):
                        rows = slice(DK * h, DK * h + DK)
                        for blk, parts in enumerate(((0, 2), (0, 3), (1, 2), (1, 3))):
                            src = qk_parts[rows, parts[0]:parts[1] + 1:parts[1] - parts[0], :]
                            sp.dma_start(stack[DK * blk:DK * blk + DK, c % 2, h].bitcast(F32),
                                         src.bitcast(F32)).then_inc(stack_in[c % 2], 16)
                    if c == 0 and more:
                        next_inputs(i)
                    if c == 1 and project:
                        next_rows(i)
                if project and not scores and not attend:
                    pass
                if project:
                    if not scores and attend:
                        next_rows(i)
                    sp.wait_ge(x1_ok, i - 1)
                    alone(sp)
                    sp.dma_start(x1_by_batch[i - 2], u_sb[:]).then_inc(x1_out, 16)

            def next_rows(i):
                sp.wait_ge(u_ok, 2 * (i - 2) + 2)
                alone(sp)
                sp.dma_start(xrow[:], x_by_batch[i - 1]).then_inc(xrow_in, 16)

            step(0, True, False, False)
            step(1, True, True, False)
            with sp.Fori(1, B // 2 - 1) as j:
                step(j * 2, True, True, True)
                step(j * 2 + 1, True, True, True)
            step(B - 2, True, True, True)
            step(B - 1, True, True, True, more=False)
            step(B, False, True, True)
            step(B + 1, False, False, True)

            sp.wait_ge(x1_out, 16 * B)
            for dst, src in ((b2_bc, b2), (l2w_bc, ln2_w), (l2b_bc, ln2_b)):
                sp.dma_start(dst[:], src.partition_broadcast(P)).then_inc(ffc_in, 16)
            sp.dma_start(b1_col[:], b1).then_inc(ffc_in, 16)
            sp.dma_start(x1[:, 0], x1_by_group[0]).then_inc(x1_in[0], 16)
            for f in range(FT):
                if f >= 2:
                    sp.wait_ge(ffw_hi_ok, 2 * (f - 1))
                    sp.wait_ge(ffw_lo_ok, 2 * (f - 1))
                sp.dma_start(w_raw[:, f % 2, 0], w1[:, f].rearrange("p k m -> p (k m)")).then_inc(ffw_in[f % 2], 16)
                sp.dma_start(w_raw[:, f % 2, 1], w2[:, f]).then_inc(ffw_in[f % 2], 16)
                if f == 4:
                    sp.dma_start(x1[:, 1], x1_by_group[1]).then_inc(x1_in[1], 16)

            def group(g, slot, first, last):
                sp.wait_ge(out_ok, g + 1)
                alone(sp)
                sp.dma_start(out_by_group[g], y_sb[:]).then_inc(out_st, 16)
                if not last:
                    sp.dma_start(x1[:, slot], x1_by_group[g + 2]).then_inc(x1_in[slot], 16)

            with sp.Fori(0, NG // 2 - 1) as j:
                group(j * 2, 0, False, False)
                group(j * 2 + 1, 1, False, False)
            group(NG - 2, 0, False, True)
            group(NG - 1, 1, False, True)
            sp.wait_ge(out_st, 16 * NG)

        @block.tensor
        def _(pe):
            def project_rows(i, quads_before):
                for t in range(RT):
                    if quads_before:
                        pe.wait_ge(qk_hi_ok, NQ * (i - 1) + 3 + t)
                        pe.wait_ge(qk_lo_ok, NQ * (i - 1) + 3 + t)
                    else:
                        pe.wait_ge(u_ok, RT * (i - 3) + t + 1)
                    if t == 0:
                        pe.wait_ge(cc_hi_ok, NQ * (i - 2) + NQ)
                        pe.wait_ge(cc_lo_ok, NQ * (i - 2) + NQ)
                    rows = slice(P * t, P * t + P)
                    for k in range(KT):
                        mm = three_passes(pe, pj_bank[t][:], cc_hi[:, k, rows], cc_lo[:, k, rows],
                                          wo_hi[:, k], wo_lo[:, k], k == 0, k == KT - 1)
                    mm.then_inc(wo_mm, 1)

            def values(i, project):
                for t in range(RT):
                    if project:
                        pe.wait_ge(u_ok, RT * (i - 2) + t + 1)
                    elif not (isinstance(i, int) and i == 0):
                        pe.wait_ge(qk_hi_ok, NQ * (i - 1) + 3 + t)
                        pe.wait_ge(qk_lo_ok, NQ * (i - 1) + 3 + t)
                    if t == 0:
                        pe.wait_ge(xc_hi_ok, 2 * i + 2)
                        pe.wait_ge(xc_lo_ok, 2 * i + 2)
                    rows = slice(P * t, P * t + P)
                    for k in range(KT):
                        mm = three_passes(pe, pj_bank[t][:], c_hi[:, k, rows], c_lo[:, k, rows],
                                          wv_hi[:, k], wv_lo[:, k], k == 0, k == KT - 1)
                    mm.then_inc(v_mm, 1)

            def queries_keys(i, c):
                if c < 2:
                    pe.wait_ge(v_ok, RT * i + c + 1)
                else:
                    pe.wait_ge(qk_hi_ok, NQ * i + c - 1)
                    pe.wait_ge(qk_lo_ok, NQ * i + c - 1)
                cols = slice(P * c, P * c + P)
                for n, (hi, lo) in enumerate(((x_hi, x_lo), (c_hi, c_lo))):
                    for k in range(KT):
                        mm = three_passes(pe, pj_bank[c % 2][:, n * S:(n + 1) * S], wk_hi[:, k, cols],
                                          wk_lo[:, k, cols], hi[:, k], lo[:, k], k == 0, k == KT - 1)
                mm.then_inc(qk_mm, 1)

            def scores(i, c, heads, attend):
                if 0 in heads:
                    pe.wait_ge(stack_in[c % 2], 512 * i + 256 * (c // 2 + 1))
                for h in heads:
                    n = HQ * c + h
                    if n >= 2 or attend:
                        pe.wait_ge(s_ok, 16 * i + n - 1)
                    dst = s_bank[h % 2]
                    q = stack[:, c % 2, h, 0]
                    k = stack[:, c % 2, h, 1]
                    nc.tensor.matmul(dst[:, 0:LATE], q[:, P:S], k, start=True, stop=True)
                    nc.tensor.matmul(dst[:, LATE:SPAN], q[:, 0:P], k[:, P:S], start=True, stop=True).then_inc(s_mm, 1)

            def transposes(i, c, heads, more):
                for h in heads:
                    n = HQ * c + h
                    pe.wait_ge(p_ok, 16 * i + n + 1)
                    if n >= 2 or more:
                        pe.wait_ge(pt_ok, 16 * i + n - 1)
                    dst = pt_bank[h % 2]
                    nc.tensor.transpose(dst[:, 0:P], p_sb[:, h, LATE:SPAN], ident[:])
                    nc.tensor.transpose(dst[:, P:S], p_sb[:, h, P:S], ident[:])
                    nc.tensor.transpose(dst[:, S:SPAN], p_sb[:, h, 0:P], ident[:]).then_inc(pt_mm, 1)

            def attend_quad(i, slot, c, more):
                pe.wait_ge(pt_ok, 16 * i + HQ * c + HQ)
                if c == 0:
                    pe.wait_ge(v_ok, RT * i + RT)
                if c >= 2 or more:
                    pe.wait_ge(cc_ok, NQ * i + c - 1)
                dst = av_bank[c % 2]
                for what in range(2):
                    at = S * what
                    for part in range(2):
                        for h in range(HQ):
                            feat = DK * (HQ * c + h)
                            rows = slice(DK * h, DK * h + DK)
                            lhs = ones[:] if what else v_sb[:, slot, 1 - part, feat:feat + DK]
                            if part == 0:
                                mm = nc.tensor.matmul(dst[rows, at:at + S], lhs, pt_sb[:, c % 2, h, 0:S],
                                                      start=True, stop=False, skip_group_check=True)
                            else:
                                mm = nc.tensor.matmul(dst[rows, at + P:at + S], lhs, pt_sb[:, c % 2, h, S:SPAN],
                                                      start=False, stop=True, skip_group_check=True)
                mm.then_inc(av_mm, 1)

            def step(i, slot, do_scores, attend, project):
                more = not (isinstance(i, int) and i == 1)
                if project:
                    project_rows(i, do_scores or attend)
                if do_scores:
                    values(i, project)
                    queries_keys(i, 0)
                    queries_keys(i, 1)
                for c in range(NQ):
                    if do_scores:
                        scores(i, c, (0, 1), attend)
                    if attend:
                        transposes(i - 1, c, (0, 1), more)
                    if do_scores and c < 2:
                        queries_keys(i, c + 2)
                    if do_scores:
                        scores(i, c, (2, 3), attend)
                    if attend:
                        transposes(i - 1, c, (2, 3), more)
                        attend_quad(i - 1, 1 - slot, c, more)

            pe.wait_ge(w_hi_ok, 3)
            pe.wait_ge(w_lo_ok, 3)
            pe.wait_ge(const_ok, CONSTS)
            step(0, 0, True, False, False)
            step(1, 1, True, True, False)
            with pe.Fori(1, B // 2) as j:
                step(j * 2, 0, True, True, True)
                step(j * 2 + 1, 1, True, True, True)
            step(B, 0, False, True, True)
            step(B + 1, 1, False, False, True)

            def turn_rows(g, slot, ks, first):
                for k in ks:
                    if k == 0:
                        pe.wait_ge(x1_in[slot], group_bytes(g, slot))
                    if first and k < 2:
                        pe.wait_ge(x1_out, 16 * B)
                    else:
                        pe.wait_ge(xt_hi_ok, KT * g + k - 1)
                        pe.wait_ge(xt_lo_ok, KT * g + k - 1)
                    for t in range(GT):
                        mm = nc.tensor.transpose(xt_bank[k % 2][:, P * t:P * t + P],
                                                 x1[:, slot, t, P * k:P * k + P], ident[:])
                    mm.then_inc(xt_mm, 1)

            def hidden(g, f, first):
                if f == 0:
                    pe.wait_ge(xt_hi_ok, KT * g + KT)
                    pe.wait_ge(xt_lo_ok, KT * g + KT)
                if f >= 2 or not first:
                    pe.wait_ge(h_ok, FT * g + f - 1)
                if first:
                    pe.wait_ge(ffw_hi_ok, 2 * f + 2)
                    pe.wait_ge(ffw_lo_ok, 2 * f + 2)
                for k in range(KT):
                    mm = three_passes(pe, h_bank[f % 2][:], w1_hi[:, f, k], w1_lo[:, f, k],
                                      xt_hi[:, k], xt_lo[:, k], k == 0, k == KT - 1)
                mm.then_inc(h_mm, 1)

            def add_hidden(g, f, first):
                pe.wait_ge(h_hi_ok, FT * g + f + 1)
                pe.wait_ge(h_lo_ok, FT * g + f + 1)
                for t in range(GT):
                    if f == 0 and not first:
                        pe.wait_ge(y_ok, GT * (g - 1) + t + 1)
                    rows = slice(P * t, P * t + P)
                    mm = three_passes(pe, y_bank[t][:], h_hi[:, f % 2, rows], h_lo[:, f % 2, rows],
                                      w2_hi[:, f], w2_lo[:, f], f == 0, f == FT - 1)
                mm.then_inc(y_step, 1)

            def group(g, slot, first, last):
                for f in range(FT):
                    hidden(g, f, first)
                    if f >= 1:
                        add_hidden(g, f - 1, first)
                if not last:
                    turn_rows(g + 1, 1 - slot, range(KT), False)
                add_hidden(g, FT - 1, first)

            turn_rows(0, 0, range(KT), True)
            over_groups(pe, group)

        @block.scalar
        def _(act):
            act.wait_ge(gam_dve, 1)
            nc.scalar.activation(g_tmp[:, 1], g_tmp[:, 0], ACT.Exp).then_inc(gam_act, 1)
            act.wait_ge(const_ok, CONSTS)
            act.wait_ge(cons_in, 16 * 6)

            def qk_high(i, c, sent):
                act.wait_ge(qk_mm, NQ * i + c + 1)
                if sent:
                    stack_sent(act, stack_in, i, c)
                nc.scalar.activation(qk_parts[:, 0:4:2], pj_bank[c % 2][:].rearrange("p (n s) -> p n s", n=2),
                                     ACT.Identity, bias=bk_col[:, c:c + 1]).then_inc(qk_hi_ok, 1)

            def first_exp(i, c, heads, attend):
                if 0 in heads:
                    act.wait_ge(nm1_ok, NQ * i + c + 1)
                    if attend:
                        act.wait_ge(p_ok, 16 * (i - 1) + HQ * c + HQ)
                for h in heads:
                    for late in (True, False):
                        a, z = head_block(c, h, late)
                        src = s_sb[:, c, h, 0:LATE] if late else s_sb[:, c, h, LATE:SPAN]
                        t = 0 if late else 1
                        e = nc.scalar.activation(w_sb[:, c, a + 1:z + 1], src, ACT.Exp, scale=SCALE,
                                                 bias=nm1[:, c, h, t:t + 1])
                if HQ - 1 in heads:
                    e.then_inc(e1_ok, 1)

            def roots(i):
                for c in range(NQ):
                    act.wait_ge(r_ok, NQ * i + c + 1)
                    nc.scalar.activation(w_sb[:, c], w_sb[:, c], ACT.Sqrt, bias=tiny[:]).then_inc(root_ok, 1)

            def effect(i, c):
                act.wait_ge(root_ok, NQ * i + c + 1)
                nc.scalar.activation(w_sb[:, c], w_sb[:, c], ACT.Exp, scale=-1.0).then_inc(te_ok, 1)

            def second_exp(i, c, more):
                act.wait_ge(nm2_ok, NQ * i + c + 1)
                for h in range(HQ):
                    if c >= 1 or more:
                        act.wait_ge(pt_mm, 16 * i + HQ * (c - 1) + h + 1)
                    for late in (True, False):
                        a, z = head_block(c, h, late)
                        dst = p_sb[:, h, 0:LATE] if late else p_sb[:, h, LATE:SPAN]
                        t = 0 if late else 1
                        e = nc.scalar.activation(dst, w_sb[:, c, a:z], ACT.Exp, scale=SCALE,
                                                 bias=nm2[:, c, h, t:t + 1])
                    e.then_inc(p_ok, 1)

            def turned(i, c, heads, more):
                for h in heads:
                    act.wait_ge(pt_mm, 16 * i + HQ * c + h + 1)
                    if h == 0 and (c >= 2 or more):
                        act.wait_ge(av_mm, NQ * i + c - 1)
                    nc.scalar.copy(pt_sb[:, c % 2, h], pt_bank[h % 2][:, 0:SPAN]).then_inc(pt_ok, 1)

            def step(i, slot, do_scores, attend, project):
                more = not (isinstance(i, int) and i == 1)
                if do_scores:
                    qk_high(i, 0, attend)
                if attend:
                    roots(i - 1)
                    effect(i - 1, 0)
                if do_scores:
                    qk_high(i, 1, True)
                for c in range(NQ):
                    if attend:
                        if c < NQ - 1:
                            effect(i - 1, c + 1)
                        second_exp(i - 1, c, more)
                    if do_scores:
                        if c < 2:
                            qk_high(i, c + 2, True)
                        first_exp(i, c, (0, 1), attend)
                    if attend:
                        turned(i - 1, c, (0, 1), more)
                    if do_scores:
                        first_exp(i, c, (2, 3), attend)
                    if attend:
                        turned(i - 1, c, (2, 3), more)

            step(0, 0, True, False, False)
            step(1, 1, True, True, False)
            with act.Fori(1, B // 2) as j:
                step(j * 2, 0, True, True, True)
                step(j * 2 + 1, 1, True, True, True)
            step(B, 0, False, True, True)

            act.wait_ge(x1_out, 16 * B)
            act.wait_ge(ffc_in, 16 * 4)

            def rows_high(g, first):
                for k in range(KT):
                    act.wait_ge(xt_mm, KT * g + k + 1)
                    if k == 0 and not first:
                        act.wait_ge(h_mm, FT * g)
                    nc.scalar.copy(xt_hi[:, k], xt_bank[k % 2][:]).then_inc(xt_hi_ok, 1)

            def group(g, slot, first, last):
                for f in range(FT):
                    act.wait_ge(h_mm, FT * g + f + 1)
                    if f >= 2 or not first:
                        act.wait_ge(h_lo_ok, FT * g + f - 1)
                    nc.scalar.activation(h_sb[:, f % 2], h_bank[f % 2][:], ACT.Relu,
                                         bias=b1_col[:, f:f + 1]).then_inc(h_ok, 1)
                    act.wait_ge(h_ok, FT * g + f + 1)
                    if f >= 2 or not first:
                        act.wait_ge(y_step, FT * g + f - 1)
                    nc.scalar.copy(h_hi[:, f % 2], h_sb[:, f % 2]).then_inc(h_hi_ok, 1)
                if not last:
                    rows_high(g + 1, False)

            rows_high(0, True)
            over_groups(act, group)

        @block.vector
        def _(dve):
            for n, hi in enumerate((wk_hi, wv_hi, wo_hi)):
                dve.wait_ge(wraw_in, 16 * 3)
                nc.vector.tensor_copy(hi[:].rearrange("p k n -> p (k n)"),
                                      s_sb_flat(s_sb)[:, n * KT * D:(n + 1) * KT * D]).then_inc(w_hi_ok, 1)

            def split_inputs(i, done):
                dve.wait_ge(xraw_in, 16 * i + 16)
                dve.wait_ge(craw_in, 16 * i + 16)
                if done:
                    dve.wait_ge(qk_mm, NQ * i)
                nc.vector.tensor_copy(x_hi[:], x_raw[:]).then_inc(xc_hi_ok, 1)
                nc.vector.tensor_copy(c_hi[:], c_raw[:]).then_inc(xc_hi_ok, 1)

            split_inputs(0, False)
            dve.wait_ge(cons_in, 16 * 6)
            chain = [0]

            def then(ins):
                chain[0] += 1
                ins.then_inc(gam_dve, 1)
                dve.wait_ge(gam_dve, chain[0])

            minus_abs, y, two_y, inv, z, zz, acc, sp = (g_tmp[:, n] for n in range(8))
            then(nc.vector.scalar_tensor_tensor(minus_abs, g_in[:], -1.0, g_in[:], ALU.mult, ALU.min))
            dve.wait_ge(gam_act, 1)
            then(nc.vector.tensor_scalar(two_y, y, 2.0, None, ALU.add))
            then(nc.vector.reciprocal(inv, two_y))
            then(nc.vector.tensor_tensor(z, y, inv, ALU.mult))
            then(nc.vector.tensor_tensor(zz, z, z, ALU.mult))
            then(nc.vector.tensor_scalar(acc, zz, 1.0 / 15, None, ALU.mult))
            for n in range(13, 1, -2):
                then(nc.vector.scalar_tensor_tensor(acc, acc, 1.0 / n, zz, ALU.add, ALU.mult))
            then(nc.vector.scalar_tensor_tensor(acc, acc, 1.0, z, ALU.add, ALU.mult))
            then(nc.vector.tensor_scalar(acc, acc, 2.0, None, ALU.mult))
            then(nc.vector.scalar_tensor_tensor(sp, g_in[:], 0.0, acc, ALU.max, ALU.add))
            for t in range(2):
                then(nc.vector.tensor_tensor(gamma2[:, :, t], sp, sp, ALU.mult))
            dve.wait_ge(const_ok, CONSTS)
            dve.wait_ge(w_lo_ok, 3)

            def qk_low(i, c):
                dve.wait_ge(qk_hi_ok, NQ * i + c + 1)
                src = pj_bank[c % 2][:].rearrange("p (n s) -> p n s", n=2)
                nc.vector.scalar_tensor_tensor(qk_parts[:, 1:4:2], src, bk_col[:, c:c + 1],
                                               qk_parts[:, 0:4:2].bitcast(F32), ALU.add,
                                               ALU.subtract).then_inc(qk_lo_ok, 1)

            def value_rows(i, slot):
                for t in range(RT):
                    dve.wait_ge(v_mm, RT * i + t + 1)
                    nc.vector.tensor_tensor(v_sb[:, slot, t], pj_bank[t][:], bv_bc[:], ALU.add).then_inc(v_ok, 1)

            def mask_scores(i, c):
                for h in range(HQ):
                    dve.wait_ge(s_mm, 16 * i + HQ * c + h + 1)
                    alone(dve)
                    nc.vector.tensor_tensor_reduce(
                        out=s_sb[:, c, h, 0:LATE], in0=s_bank[h % 2][:, 0:LATE], in1=mask[:],
                        scale=1.0, scalar=NEG, op0=ALU.add, op1=ALU.max, accum_out=m1[:, c, h, 0:1])
                    nc.vector.tensor_tensor_reduce(
                        out=s_sb[:, c, h, LATE:SPAN], in0=s_bank[h % 2][:, LATE:SPAN], in1=mask[:, 0:EARLY],
                        scale=1.0, scalar=NEG, op0=ALU.add, op1=ALU.max,
                        accum_out=m1[:, c, h, 1:2]).then_inc(s_ok, 1)
                dve.wait_ge(s_ok, 16 * i + HQ * c + HQ)
                nc.vector.tensor_scalar(nm1[:, c], m1[:, c], -SCALE, None, ALU.mult).then_inc(nm1_ok, 1)

            def running_sums(i, c):
                dve.wait_ge(e1_ok, NQ * i + c + 1)
                blocks = w_sb[:, c].rearrange("p (h w) -> p h w", h=HQ)
                nc.vector.memset(blocks[:, :, 0:LATE + 2:LATE + 1], 0.0).then_inc(zero_ok, 1)
                dve.wait_ge(zero_ok, NQ * i + c + 1)
                nc.vector.tensor_tensor_scan(w_sb[:, c], carry[:], w_sb[:, c], 0.0,
                                             ALU.mult, ALU.add).then_inc(scan_ok, 1)
                dve.wait_ge(scan_ok, NQ * i + c + 1)
                nc.vector.reciprocal(zi[:, c], blocks[:, :, LATE:BLK:EARLY + 1]).then_inc(zi_ok, 1)
                dve.wait_ge(zi_ok, NQ * i + c + 1)
                nc.vector.tensor_tensor(gz[:, c], zi[:, c], gamma2[:, HQ * c:HQ * c + HQ],
                                        ALU.mult).then_inc(gz_ok, 1)

            def decay(i, c):
                dve.wait_ge(t_ok, NQ * i + c + 1)
                dve.wait_ge(gz_ok, NQ * i + c + 1)
                for h in range(HQ):
                    for t in range(2):
                        a, z = head_block(c, h, t == 0)
                        r = nc.vector.tensor_scalar(w_sb[:, c, a:z], w_sb[:, c, a:z], gz[:, c, h, t:t + 1],
                                                    R_MAX, ALU.mult, ALU.min)
                r.then_inc(r_ok, 1)

            def decayed_scores(i, c):
                dve.wait_ge(te_ok, NQ * i + c + 1)
                alone(dve)
                for h in range(HQ):
                    for t in range(2):
                        a, z = head_block(c, h, t == 0)
                        src = s_sb[:, c, h, 0:LATE] if t == 0 else s_sb[:, c, h, LATE:SPAN]
                        r = nc.vector.tensor_tensor_reduce(
                            out=w_sb[:, c, a:z], in0=w_sb[:, c, a:z], in1=src, scale=1.0, scalar=NEG,
                            op0=ALU.mult, op1=ALU.max, accum_out=m2[:, c, h, t:t + 1])
                r.then_inc(s2_ok, 1)
                dve.wait_ge(s2_ok, NQ * i + c + 1)
                nc.vector.tensor_scalar(nm2[:, c], m2[:, c], -SCALE, None, ALU.mult).then_inc(nm2_ok, 1)

            def concat(i, c, more):
                dve.wait_ge(av_mm, NQ * i + c + 1)
                if c >= 1 or more:
                    dve.wait_ge(cc_ok, NQ * i + c)
                nc.vector.reciprocal(zr_sb[:], av_bank[c % 2][:, S:2 * S]).then_inc(zr_ok, 1)
                dve.wait_ge(zr_ok, NQ * i + c + 1)
                if c >= 2 or more:
                    dve.wait_ge(cc_lo_ok, NQ * i + c - 1)
                nc.vector.tensor_tensor(cc_sb[:, c % 2], av_bank[c % 2][:, 0:S], zr_sb[:],
                                        ALU.mult).then_inc(cc_ok, 1)

            def residual(i):
                dve.wait_ge(xb_ok, i + 1)
                if not (isinstance(i, int) and i == 0):
                    dve.wait_ge(x1_out, 16 * i)
                for t in range(RT):
                    dve.wait_ge(wo_mm, RT * i + t + 1)
                    nc.vector.tensor_tensor(u_sb[:, t], pj_bank[t][:], xrow[:, t], ALU.add).then_inc(u_ok, 1)

            def moments(i):
                for t in range(RT):
                    dve.wait_ge(u_ok, RT * i + t + 1)
                    nc.vector.bn_stats(bn1[:, t], u_sb[:, t]).then_inc(bn1_ok, 1)
                for t in range(RT):
                    dve.wait_ge(bn1_ok, RT * i + t + 1)
                    alone(dve)
                    nc.vector.bn_aggr(mv1[:, t], bn1[:, t]).then_inc(mv1_ok, 1)

            def normalise(i):
                dve.wait_ge(rstd1_ok, i + 1)
                for t in range(RT):
                    nc.vector.tensor_scalar(u_sb[:, t], u_sb[:, t], mv1[:, t, 0:1], rstd1[:, t:t + 1],
                                            ALU.subtract, ALU.mult).then_inc(norm1_ok, 1)

            def step(i, slot, do_scores, attend, project, split=True):
                more = not (isinstance(i, int) and i == 1)
                if project:
                    residual(i - 2)
                if do_scores:
                    value_rows(i, slot)
                    qk_low(i, 0)
                if project:
                    moments(i - 2)
                for c in range(NQ):
                    if attend:
                        decayed_scores(i - 1, c)
                    if do_scores and c == 0:
                        qk_low(i, 1)
                    if do_scores and c >= 2:
                        decay(i, c - 2)
                    if do_scores and c >= 1:
                        running_sums(i, c - 1)
                    if do_scores:
                        mask_scores(i, c)
                    if attend and c >= 1:
                        concat(i - 1, c - 1, more or c >= 2)
                    if do_scores and c in (1, 2):
                        qk_low(i, c + 1)
                    if project and c == 0:
                        normalise(i - 2)
                    if do_scores and split and c == 3:
                        split_inputs(i + 1, True)
                if do_scores:
                    running_sums(i, 3)
                    decay(i, 2)
                    decay(i, 3)
                if attend:
                    concat(i - 1, 3, True)

            step(0, 0, True, False, False)
            step(1, 1, True, True, False)
            with dve.Fori(1, B // 2 - 1) as j:
                step(j * 2, 0, True, True, True)
                step(j * 2 + 1, 1, True, True, True)
            step(B - 2, 0, True, True, True)
            step(B - 1, 1, True, True, True, split=False)
            step(B, 0, False, True, True)
            step(B + 1, 1, False, False, True)

            dve.wait_ge(x1_out, 16 * B)
            dve.wait_ge(ffc_in, 16 * 4)

            def weights_high(f):
                dve.wait_ge(ffw_in[f % 2], 32 * (f // 2 + 1))
                nc.vector.tensor_copy(w1_hi[:, f].rearrange("p k m -> p (k m)"), w_raw[:, f % 2, 0]).then_inc(ffw_hi_ok, 1)
                nc.vector.tensor_copy(w2_hi[:, f], w_raw[:, f % 2, 1]).then_inc(ffw_hi_ok, 1)

            def rows_low(g):
                for k in range(KT):
                    dve.wait_ge(xt_hi_ok, KT * g + k + 1)
                    nc.vector.tensor_tensor(xt_lo[:, k], xt_bank[k % 2][:], xt_hi[:, k].bitcast(F32),
                                            ALU.subtract).then_inc(xt_lo_ok, 1)

            def group(g, slot, first, last):
                for f in range(FT):
                    if first and f + 2 < FT:
                        weights_high(f + 2)
                    dve.wait_ge(h_hi_ok, FT * g + f + 1)
                    nc.vector.tensor_tensor(h_lo[:, f % 2], h_sb[:, f % 2], h_hi[:, f % 2].bitcast(F32),
                                            ALU.subtract).then_inc(h_lo_ok, 1)
                if not last:
                    rows_low(g + 1)
                dve.wait_ge(y_step, FT * g + FT)
                dve.wait_ge(xb2_ok, g + 1)
                if not first:
                    dve.wait_ge(out_st, 16 * g)
                for t in range(GT):
                    nc.vector.tensor_tensor(y_sb[:, t], y_bank[t][:], x1[:, slot, t], ALU.add).then_inc(y_ok, 1)
                for t in range(GT):
                    dve.wait_ge(y_ok, GT * g + t + 1)
                    nc.vector.bn_stats(bn2[:, t], y_sb[:, t]).then_inc(bn2_ok, 1)
                for t in range(GT):
                    dve.wait_ge(bn2_ok, GT * g + t + 1)
                    alone(dve)
                    nc.vector.bn_aggr(mv2[:, t], bn2[:, t]).then_inc(mv2_ok, 1)
                dve.wait_ge(rstd2_ok, g + 1)
                for t in range(GT):
                    nc.vector.tensor_scalar(y_sb[:, t], y_sb[:, t], mv2[:, t, 0:1], rstd2[:, t:t + 1],
                                            ALU.subtract, ALU.mult).then_inc(norm2_ok, 1)

            weights_high(0)
            weights_high(1)
            rows_low(0)
            over_groups(dve, group)

        @block.gpsimd
        def _(pool):
            nc.gpsimd.iota(iota_i[:], pattern=[[1, S]], base=1 - P, channel_multiplier=1).then_inc(const_ok, 1)
            nc.gpsimd.memset(mask[:], 0.0).then_inc(const_ok, 1)
            nc.gpsimd.memset(ident[:], 0.0).then_inc(const_ok, 1)
            nc.gpsimd.memset(carry[:], 1.0).then_inc(const_ok, 1)
            nc.gpsimd.memset(ones[:], 1.0).then_inc(const_ok, 1)
            nc.gpsimd.memset(half[:], -0.5).then_inc(const_ok, 1)
            nc.gpsimd.memset(tiny[:], R_TINY).then_inc(const_ok, 1)
            pool.wait_ge(const_ok, 7)
            nc.gpsimd.tensor_copy(dist[:], iota_i[:]).then_inc(const_ok, 1)
            nc.gpsimd.affine_select(out=mask[:], in_=mask[:], compare_op=ALU.is_ge, fill=NEG, base=1 - P,
                                    pattern=[[1, S]], channel_multiplier=1).then_inc(const_ok, 1)
            nc.gpsimd.affine_select(out=ident[:], in_=ident[:], compare_op=ALU.not_equal, fill=1.0, base=0,
                                    pattern=[[-1, P]], channel_multiplier=1).then_inc(const_ok, 1)
            nc.gpsimd.memset(carry[:].rearrange("p (h w) -> p h w", h=HQ)[:, :, 0:LATE + 2:LATE + 1],
                             0.0).then_inc(const_ok, 1)
            for n, (hi, lo) in enumerate(((wk_hi, wk_lo), (wv_hi, wv_lo), (wo_hi, wo_lo))):
                pool.wait_ge(w_hi_ok, n + 1)
                nc.gpsimd.tensor_tensor(lo[:].rearrange("p k n -> p (k n)"),
                                        s_sb_flat(s_sb)[:, n * KT * D:(n + 1) * KT * D],
                                        hi[:].rearrange("p k n -> p (k n)").bitcast(F32),
                                        ALU.subtract).then_inc(w_lo_ok, 1)

            def split_inputs(i):
                for n, (raw, hi, lo) in enumerate(((x_raw, x_hi, x_lo), (c_raw, c_hi, c_lo))):
                    pool.wait_ge(xc_hi_ok, 2 * i + n + 1)
                    nc.gpsimd.tensor_tensor(lo[:], raw[:], hi[:].bitcast(F32), ALU.subtract).then_inc(xc_lo_ok, 1)

            split_inputs(0)
            pool.wait_ge(const_ok, CONSTS)
            pool.wait_ge(cons_in, 16 * 6)

            def add_bias(i):
                pool.wait_ge(xrow_in, 16 * i + 16)
                nc.gpsimd.tensor_tensor(xrow[:], xrow[:], bo_bc[:].unsqueeze(1).broadcast_to([P, RT, D]),
                                        ALU.add).then_inc(xb_ok, 1)

            def times_distance(i, c):
                pool.wait_ge(scan_ok, NQ * i + c + 1)
                blocks = w_sb[:, c].rearrange("p (h w) -> p h w", h=HQ)
                nc.gpsimd.tensor_tensor(blocks[:, :, 0:LATE], blocks[:, :, 0:LATE],
                                        dist[:].unsqueeze(1).broadcast_to([P, HQ, LATE]), ALU.mult)
                nc.gpsimd.tensor_tensor(blocks[:, :, LATE + 1:BLK - 1], blocks[:, :, LATE + 1:BLK - 1],
                                        dist[:, 0:EARLY].unsqueeze(1).broadcast_to([P, HQ, EARLY]),
                                        ALU.mult).then_inc(t_ok, 1)

            def split_concat(i, c, more):
                pool.wait_ge(cc_ok, NQ * i + c + 1)
                if c == 0 and more:
                    pool.wait_ge(wo_mm, RT * i)
                alone(pool)
                nc.gpsimd.tensor_copy(cc_hi[:, c], cc_sb[:, c % 2]).then_inc(cc_hi_ok, 1)
                pool.wait_ge(cc_hi_ok, NQ * i + c + 1)
                nc.gpsimd.tensor_tensor(cc_lo[:, c], cc_sb[:, c % 2], cc_hi[:, c].bitcast(F32),
                                        ALU.subtract).then_inc(cc_lo_ok, 1)

            def deviation(i):
                pool.wait_ge(mv1_ok, RT * i + RT)
                alone(pool)
                nc.gpsimd.tensor_scalar(rstd1[:], mv1[:, :, 1], EPS_LN, None, ALU.add).then_inc(ve1_ok, 1)
                pool.wait_ge(ve1_ok, i + 1)
                nc.gpsimd.tensor_tensor(rstd1[:], rstd1[:], half[:, 0:RT], ALU.pow).then_inc(rstd1_ok, 1)

            def scale_shift(i):
                pool.wait_ge(norm1_ok, RT * i + RT)
                nc.gpsimd.tensor_tensor(u_sb[:], u_sb[:], l1w_bc[:].unsqueeze(1).broadcast_to([P, RT, D]),
                                        ALU.mult).then_inc(scaled1_ok, 1)
                pool.wait_ge(scaled1_ok, i + 1)
                nc.gpsimd.tensor_tensor(u_sb[:], u_sb[:], l1b_bc[:].unsqueeze(1).broadcast_to([P, RT, D]),
                                        ALU.add).then_inc(x1_ok, 1)

            def step(i, slot, do_scores, attend, project, split=True):
                more = not (isinstance(i, int) and i == 1)
                if project:
                    deviation(i - 2)
                for c in range(NQ):
                    if do_scores and c >= 1:
                        times_distance(i, c - 1)
                    if c == 1 and project:
                        scale_shift(i - 2)
                    if attend and c >= 1:
                        split_concat(i - 1, c - 1, more)
                if do_scores and split:
                    split_inputs(i + 1)
                if do_scores:
                    times_distance(i, 3)
                if attend:
                    split_concat(i - 1, 3, more)
                    add_bias(i - 1)

            step(0, 0, True, False, False)
            step(1, 1, True, True, False)
            with pool.Fori(1, B // 2 - 1) as j:
                step(j * 2, 0, True, True, True)
                step(j * 2 + 1, 1, True, True, True)
            step(B - 2, 0, True, True, True)
            step(B - 1, 1, True, True, True, split=False)
            step(B, 0, False, True, True)
            step(B + 1, 1, False, False, True)

            pool.wait_ge(x1_out, 16 * B)
            pool.wait_ge(ffc_in, 16 * 4)

            def weights_low(f):
                pool.wait_ge(ffw_hi_ok, 2 * f + 2)
                nc.gpsimd.tensor_tensor(w1_lo[:, f].rearrange("p k m -> p (k m)"), w_raw[:, f % 2, 0],
                                        w1_hi[:, f].rearrange("p k m -> p (k m)").bitcast(F32),
                                        ALU.subtract).then_inc(ffw_lo_ok, 1)
                nc.gpsimd.tensor_tensor(w2_lo[:, f], w_raw[:, f % 2, 1], w2_hi[:, f].bitcast(F32),
                                        ALU.subtract).then_inc(ffw_lo_ok, 1)

            def group(g, slot, first, last):
                if first:
                    for f in range(2, FT):
                        weights_low(f)
                pool.wait_ge(xt_mm, KT * g + KT)
                nc.gpsimd.tensor_tensor(x1[:, slot], x1[:, slot], b2_bc[:].unsqueeze(1).broadcast_to([P, GT, D]),
                                        ALU.add).then_inc(xb2_ok, 1)
                pool.wait_ge(mv2_ok, GT * g + GT)
                alone(pool)
                nc.gpsimd.tensor_scalar(rstd2[:], mv2[:, :, 1], EPS_LN, None, ALU.add).then_inc(ve2_ok, 1)
                pool.wait_ge(ve2_ok, g + 1)
                nc.gpsimd.tensor_tensor(rstd2[:], rstd2[:], half[:], ALU.pow).then_inc(rstd2_ok, 1)
                pool.wait_ge(norm2_ok, GT * g + GT)
                nc.gpsimd.tensor_tensor(y_sb[:], y_sb[:], l2w_bc[:].unsqueeze(1).broadcast_to([P, GT, D]),
                                        ALU.mult).then_inc(scaled2_ok, 1)
                pool.wait_ge(scaled2_ok, g + 1)
                nc.gpsimd.tensor_tensor(y_sb[:], y_sb[:], l2b_bc[:].unsqueeze(1).broadcast_to([P, GT, D]),
                                        ALU.add).then_inc(out_ok, 1)

            weights_low(0)
            weights_low(1)
            over_groups(pool, group)


CONSTS = 11


def s_sb_flat(s_sb):
    return s_sb[:].rearrange("p c h w -> p (c h w)")


def group_bytes(g, slot):
    return 16 * (g // 2 + 1) if isinstance(g, int) else 8 * (g - slot) + 16


def stack_sent(act, stack_in, i, c):
    if c == 0:
        act.wait_ge(stack_in[1], 512 * i)
    else:
        act.wait_ge(stack_in[(c - 1) % 2], 512 * i + 256 * ((c - 1) // 2 + 1))


def kernel(**inputs):
    import numpy as np
    import concourse.bacc as bacc
    from concourse.bass_utils import run_bass_kernel_spmd

    a = {k.removeprefix("L0_xattn_"): np.asarray(v) for k, v in inputs.items()}
    x, ctx = a["x"], a["ctx_1024"]
    B, S, D = x.shape
    F = a["b1"].shape[0]
    kt, ft = D // P, F // P

    def features_first(t):
        return t.reshape(B, S, kt, P).transpose(0, 3, 2, 1)

    def weight(w):
        return w.reshape(w.shape[0], w.shape[1] // P, P).transpose(2, 1, 0)

    arrays = {
        "x_rows": x, "x_t": features_first(x), "ctx_t": features_first(ctx[:, ::-1]),
        "wk": weight(a["Wk"]), "bk": a["bk"].reshape(kt, P).transpose(1, 0),
        "wv": weight(a["Wv"]), "bv": a["bv"], "wo": weight(a["Wo"]), "bo": a["bo"],
        "gammas": a["gammas"].reshape(-1), "ln1_w": a["ln1_w"], "ln1_b": a["ln1_b"],
        "w1": a["W1"].reshape(ft, P, kt, P).transpose(3, 0, 2, 1), "b1": a["b1"].reshape(ft, P).transpose(1, 0),
        "w2": weight(a["W2"]), "b2": a["b2"], "ln2_w": a["ln2_w"], "ln2_b": a["ln2_b"],
    }
    arrays = {k: np.ascontiguousarray(v) for k, v in arrays.items()}
    nc = bacc.Bacc("TRN2", target_bir_lowering=False, num_devices=1)
    aps = [nc.dram_tensor(k, v.shape, mybir.dt.from_np(v.dtype), kind="ExternalInput").ap()
           for k, v in arrays.items()]
    out = nc.dram_tensor("out", (B, S, D), F32, kind="ExternalOutput").ap()
    build(nc, *aps, out)
    r = run_bass_kernel_spmd(nc, [arrays], core_ids=[0])
    return r.results[0]["out"]
```

```python
from contextlib import ExitStack

import concourse.bass as bass
from concourse import mybir

F32 = mybir.dt.float32
F32R = mybir.dt.float32r
I32 = mybir.dt.int32
ALU = mybir.AluOpType
ACT = mybir.ActivationFunctionType
AX_X = mybir.AxisListType.X

P = 128
NEG = -1e32
EPS_LN = 1e-5
R_MAX = 132.54745276195996
R_TINY = 1e-30


def build(nc, x_rows, x_t, ctx_t, wk, bk, wv, bv, wo, bo, gammas, ln1_w, ln1_b,
          w1, b1, w2, b2, ln2_w, ln2_b, out):
    B, S, D = x_rows.shape
    H = gammas.shape[0]
    F = b1.shape[1] * P
    DK = D // H
    KT = D // P
    RT = S // P
    NQ = D // P
    HQ = P // DK
    FT = F // P
    SCALE = 1.0 / float(DK) ** 0.5
    assert RT == 2 and HQ == 4 and NQ == 4
    LATE, EARLY = S, P
    SPAN = LATE + EARLY
    BLK = SPAN + 2
    QW = HQ * BLK
    GR = 512
    GT = GR // P
    NG = B * S // GR

    x1_dram = nc.dram_tensor("x1_rows", (B * S, D), F32, kind="Internal").ap()
    x1_by_batch = x1_dram.rearrange("(b t p) n -> b p t n", b=B, p=P)
    x1_by_group = x1_dram.rearrange("(g t p) n -> g p t n", g=NG, p=P)
    x_by_batch = x_rows.rearrange("b (t p) n -> b p t n", p=P)
    out_by_group = out.rearrange("b s n -> (b s) n").rearrange("(g t p) n -> g p t n", g=NG, p=P)

    with ExitStack() as whole:
        def sem(name):
            return whole.enter_context(nc.semaphore(name))

        def tensor(stack, name, shape, dt=F32):
            return stack.enter_context(nc.sbuf_tensor(name, shape, dt))

        bank = [whole.enter_context(nc.psum_tensor(f"bank{i}", [P, 512], F32)) for i in range(8)]

        ident = tensor(whole, "ident", [P, P])
        half = tensor(whole, "minus_half", [P, GT])
        tiny = tensor(whole, "tiny", [P, 1])

        ph1 = ExitStack()
        wk_hi, wk_lo, wv_hi, wv_lo, wo_hi, wo_lo = (
            tensor(ph1, n, [P, KT, D], F32R) for n in ("wk_hi", "wk_lo", "wv_hi", "wv_lo", "wo_hi", "wo_lo"))
        x_raw = tensor(ph1, "x_raw", [P, KT, S])
        c_raw = tensor(ph1, "c_raw", [P, KT, S])
        x_hi, x_lo, c_hi, c_lo = (tensor(ph1, n, [P, KT, S], F32R) for n in ("x_hi", "x_lo", "c_hi", "c_lo"))
        qk_parts = tensor(ph1, "qk_parts", [P, 2, 4, S], F32R)
        q_alone = tensor(ph1, "q_alone", [P, 2, 2, HQ, S], F32R)
        v_sb = tensor(ph1, "v_sb", [P, 2, RT, D])
        s_sb = tensor(ph1, "s_sb", [P, NQ, HQ, SPAN])
        w_sb = tensor(ph1, "w_sb", [P, NQ, QW])
        p_sb = tensor(ph1, "p_sb", [P, HQ, SPAN])
        pt_sb = tensor(ph1, "pt_sb", [P, 2, HQ, SPAN])
        zi_wide = tensor(ph1, "zi_wide", [P, 2, HQ, DK])
        cc_sb = tensor(ph1, "cc_sb", [P, 2, S])
        cc_hi = tensor(ph1, "cc_hi", [P, NQ, S], F32R)
        cc_lo = tensor(ph1, "cc_lo", [P, NQ, S], F32R)
        xrow = tensor(ph1, "xrow", [P, RT, D])
        u_sb = tensor(ph1, "u_sb", [P, RT, D])
        bv_bc, bo_bc, l1w_bc, l1b_bc = (tensor(ph1, n, [P, D]) for n in ("bv_bc", "bo_bc", "l1w_bc", "l1b_bc"))
        bk_col = tensor(ph1, "bk_col", [P, NQ])
        dist = tensor(ph1, "dist", [P, S])
        mask = tensor(ph1, "mask", [P, S])
        carry = tensor(ph1, "carry", [P, QW])
        g_in = tensor(ph1, "g_in", [P, H])
        gamma2 = tensor(ph1, "gamma2", [P, H, 2])
        m1, nm1, zi, gz, m2, nm2, z2 = (
            tensor(ph1, n, [P, NQ, HQ, 2]) for n in ("m1", "nm1", "zi", "gz", "m2", "nm2", "z2"))
        bn1 = tensor(ph1, "bn1", [P, RT, 6])
        iota_i = cc_sb[:, 0].bitcast(I32)
        g_tmp = cc_sb[:, 1, 0:8 * H].rearrange("p (n h) -> p n h", n=8)
        mv1 = tensor(ph1, "mv1", [P, RT, 2])
        rstd1 = tensor(ph1, "rstd1", [P, RT])
        ph1.close()

        w1_hi, w1_lo = (tensor(whole, n, [P, FT, KT, P], F32R) for n in ("w1_hi", "w1_lo"))
        w2_hi, w2_lo = (tensor(whole, n, [P, FT, D], F32R) for n in ("w2_hi", "w2_lo"))
        w_raw = tensor(whole, "w_raw", [P, 2, 2, 512])
        x1 = tensor(whole, "x1", [P, 2, GT, D])
        xt_hi, xt_lo = (tensor(whole, n, [P, KT, GR], F32R) for n in ("xt_hi", "xt_lo"))
        h_sb = tensor(whole, "h_sb", [P, 2, GR])
        h_hi, h_lo = (tensor(whole, n, [P, 2, GR], F32R) for n in ("h_hi", "h_lo"))
        y_sb = tensor(whole, "y_sb", [P, GT, D])
        b2_bc, l2w_bc, l2b_bc = (tensor(whole, n, [P, D]) for n in ("b2_bc", "l2w_bc", "l2b_bc"))
        b1_col = tensor(whole, "b1_col", [P, FT])
        bn2 = tensor(whole, "bn2", [P, GT, 6])
        mv2 = tensor(whole, "mv2", [P, GT, 2])
        rstd2 = tensor(whole, "rstd2", [P, GT])

        wraw_in = sem("wraw_in")
        cons_in = sem("cons_in")
        const_ok = sem("const_ok")
        w_hi_ok = sem("w_hi_ok")
        w_lo_ok = sem("w_lo_ok")
        gam_act = sem("gam_act")
        gam_dve = sem("gam_dve")
        xraw_in = sem("xraw_in")
        craw_in = sem("craw_in")
        xrow_in = sem("xrow_in")
        xc_hi_ok = sem("xc_hi_ok")
        xc_lo_ok = sem("xc_lo_ok")
        qk_mm = sem("qk_mm")
        v_mm = sem("v_mm")
        wo_mm = sem("wo_mm")
        qk_hi_ok = sem("qk_hi_ok")
        qk_lo_ok = sem("qk_lo_ok")
        q_in = [sem(f"q_in{n}") for n in range(2)]
        v_ok = sem("v_ok")
        s_mm = sem("s_mm")
        s_ok = sem("s_ok")
        nm1_ok = sem("nm1_ok")
        e1_ok = sem("e1_ok")
        zero_ok = sem("zero_ok")
        scan_ok = sem("scan_ok")
        zi_ok = sem("zi_ok")
        gz_ok = sem("gz_ok")
        t_ok = sem("t_ok")
        r_ok = sem("r_ok")
        root_ok = sem("root_ok")
        te_ok = sem("te_ok")
        s2_ok = sem("s2_ok")
        nm2_ok = sem("nm2_ok")
        p_ok = sem("p_ok")
        pt_mm = sem("pt_mm")
        pt_ok = sem("pt_ok")
        av_mm = sem("av_mm")
        zi2_ok = sem("zi2_ok")
        zi_row_ok = sem("zi_row_ok")
        wide_ok = sem("wide_ok")
        cc_ok = sem("cc_ok")
        cc_hi_ok = sem("cc_hi_ok")
        cc_lo_ok = sem("cc_lo_ok")
        xb_ok = sem("xb_ok")
        u_ok = sem("u_ok")
        bn1_ok = sem("bn1_ok")
        mv1_ok = sem("mv1_ok")
        ve1_ok = sem("ve1_ok")
        rstd1_ok = sem("rstd1_ok")
        norm1_ok = sem("norm1_ok")
        scaled1_ok = sem("scaled1_ok")
        x1_ok = sem("x1_ok")
        x1_out = sem("x1_out")

        ffw_in = [sem(f"ffw_in{n}") for n in range(2)]
        ffw_hi_ok = sem("ffw_hi_ok")
        ffw_lo_ok = sem("ffw_lo_ok")
        ffc_in = sem("ffc_in")
        x1_in = [sem(f"x1_in{n}") for n in range(2)]
        xt_mm = sem("xt_mm")
        xt_hi_ok = sem("xt_hi_ok")
        xt_lo_ok = sem("xt_lo_ok")
        h_mm = sem("h_mm")
        h_ok = sem("h_ok")
        h_hi_ok = sem("h_hi_ok")
        h_lo_ok = sem("h_lo_ok")
        y_step = sem("y_step")
        xb2_ok = sem("xb2_ok")
        y_ok = sem("y_ok")
        bn2_ok = sem("bn2_ok")
        mv2_ok = sem("mv2_ok")
        ve2_ok = sem("ve2_ok")
        rstd2_ok = sem("rstd2_ok")
        norm2_ok = sem("norm2_ok")
        scaled2_ok = sem("scaled2_ok")
        out_ok = sem("out_ok")
        out_st = sem("out_st")

        s_bank, pt_bank, av_bank, pj_bank = bank[0:2], bank[2:5], bank[5], bank[6:8]
        y_bank, h_bank, xt_bank = bank[0:4], bank[4:6], bank[6:8]

        def head_block(c, h, late):
            at = h * BLK + (0 if late else LATE + 1)
            return at, at + (LATE if late else EARLY)

        def three_passes(pe, dst, a_hi, a_lo, b_hi, b_lo, start, stop):
            nc.tensor.matmul(dst, a_hi, b_hi, start=start, stop=False)
            nc.tensor.matmul(dst, a_hi, b_lo, start=False, stop=False)
            return nc.tensor.matmul(dst, a_lo, b_hi, start=False, stop=stop)

        def over_batches(engine, step):
            step(0, 0, True, False, False, True, True)
            step(1, 1, True, True, False, True, True)
            with engine.Fori(1, B // 2 - 1) as j:
                step(j * 2, 0, True, True, True, True, True)
                step(j * 2 + 1, 1, True, True, True, True, True)
            step(B - 2, 0, True, True, True, True, False)
            step(B - 1, 1, True, True, True, False, False)
            step(B, 0, False, True, True, False, False)
            step(B + 1, 1, False, False, True, False, False)

        def over_groups(engine, group):
            group(0, 0, True, False)
            with engine.Fori(1, NG // 2) as j:
                group(j * 2 - 1, 1, False, False)
                group(j * 2, 0, False, False)
            group(NG - 1, 1, False, True)

        carried = sem("carried")

        def alone(engine):
            engine.sem_inc(carried)

        block = whole.enter_context(nc.Block())

        @block.sync
        def _(sp):
            for n, w in enumerate((wk, wv, wo)):
                sp.dma_start(s_sb_flat(s_sb)[:, n * KT * D:(n + 1) * KT * D],
                             w.rearrange("p k n -> p (k n)")).then_inc(wraw_in, 16)
            sp.dma_start(x_raw[:], x_t[0]).then_inc(xraw_in, 16)
            sp.dma_start(c_raw[:], ctx_t[0]).then_inc(craw_in, 16)
            for dst, src in ((bv_bc, bv), (bo_bc, bo), (l1w_bc, ln1_w), (l1b_bc, ln1_b), (g_in, gammas)):
                sp.dma_start(dst[:], src.partition_broadcast(P)).then_inc(cons_in, 16)
            sp.dma_start(bk_col[:], bk).then_inc(cons_in, 16)
            sp.dma_start(xrow[:], x_by_batch[0]).then_inc(xrow_in, 16)

            def inputs(i):
                sp.wait_ge(xc_lo_ok, 2 * i)
                alone(sp)
                sp.dma_start(x_raw[:], x_t[i]).then_inc(xraw_in, 16)
                sp.dma_start(c_raw[:], ctx_t[i]).then_inc(craw_in, 16)

            def queries(i, c):
                sp.wait_ge(qk_lo_ok, NQ * i + c + 1)
                for h in range(HQ):
                    rows = slice(DK * h, DK * h + DK)
                    sp.dma_start(q_alone[rows, c % 2, :, h].bitcast(F32),
                                 qk_parts[rows, c % 2, 0:2].bitcast(F32)).then_inc(q_in[c % 2], 16)

            def rows_of(i):
                sp.wait_ge(u_ok, RT * i)
                alone(sp)
                sp.dma_start(xrow[:], x_by_batch[i]).then_inc(xrow_in, 16)

            def step(i, slot, now, last, older, ahead, load):
                if now:
                    queries(i, 1)
                    queries(i, 2)
                    queries(i, 3)
                if load:
                    inputs(i + 2)
                if older and last:
                    rows_of(i - 1)
                if ahead:
                    queries(i + 1, 0)
                if older:
                    sp.wait_ge(x1_ok, i - 1)
                    alone(sp)
                    sp.dma_start(x1_by_batch[i - 2], u_sb[:]).then_inc(x1_out, 16)

            inputs(1)
            sp.wait_ge(const_ok, CONSTS)
            queries(0, 0)
            over_batches(sp, step)

            sp.wait_ge(x1_out, 16 * B)
            for dst, src in ((b2_bc, b2), (l2w_bc, ln2_w), (l2b_bc, ln2_b)):
                sp.dma_start(dst[:], src.partition_broadcast(P)).then_inc(ffc_in, 16)
            sp.dma_start(b1_col[:], b1).then_inc(ffc_in, 16)
            sp.dma_start(x1[:, 0], x1_by_group[0]).then_inc(x1_in[0], 16)
            for f in range(FT):
                if f >= 2:
                    sp.wait_ge(ffw_hi_ok, 2 * (f - 1))
                    sp.wait_ge(ffw_lo_ok, 2 * (f - 1))
                sp.dma_start(w_raw[:, f % 2, 0], w1[:, f].rearrange("p k m -> p (k m)")).then_inc(ffw_in[f % 2], 16)
                sp.dma_start(w_raw[:, f % 2, 1], w2[:, f]).then_inc(ffw_in[f % 2], 16)
                if f == 4:
                    sp.dma_start(x1[:, 1], x1_by_group[1]).then_inc(x1_in[1], 16)

            def group(g, slot, more):
                sp.wait_ge(out_ok, GT * g + GT)
                alone(sp)
                sp.dma_start(out_by_group[g], y_sb[:]).then_inc(out_st, 16)
                if more:
                    sp.dma_start(x1[:, slot], x1_by_group[g + 2]).then_inc(x1_in[slot], 16)

            with sp.Fori(0, NG // 2 - 1) as j:
                group(j * 2, 0, True)
                group(j * 2 + 1, 1, True)
            group(NG - 2, 0, False)
            for t in range(GT):
                sp.wait_ge(out_ok, GT * (NG - 1) + t + 1)
                sp.dma_start(out_by_group[NG - 1, :, t], y_sb[:, t]).then_inc(out_st, 16)
            sp.wait_ge(out_st, 16 * (NG - 1 + GT))

        @block.tensor
        def _(pe):
            def project_rows(i, t, now):
                if now and t == 0:
                    pe.wait_ge(v_ok, RT * i + 2)
                elif now:
                    pe.wait_ge(qk_lo_ok, NQ * i + 4)
                else:
                    pe.wait_ge(u_ok, RT * (i - 3) + t + 1)
                if t == 0:
                    pe.wait_ge(cc_lo_ok, NQ * (i - 2) + NQ)
                rows = slice(P * t, P * t + P)
                for k in range(KT):
                    mm = three_passes(pe, pj_bank[t][:], cc_hi[:, k, rows], cc_lo[:, k, rows],
                                      wo_hi[:, k], wo_lo[:, k], k == 0, k == KT - 1)
                mm.then_inc(wo_mm, 1)

            def values(i, t):
                pe.wait_ge(qk_lo_ok, NQ * i + 2 + t)
                rows = slice(P * t, P * t + P)
                for k in range(KT):
                    mm = three_passes(pe, pj_bank[1 - t][:], c_hi[:, k, rows], c_lo[:, k, rows],
                                      wv_hi[:, k], wv_lo[:, k], k == 0, k == KT - 1)
                mm.then_inc(v_mm, 1)

            def queries_keys(i, c, before):
                if c == 2:
                    pe.wait_ge(qk_lo_ok, NQ * i + 1)
                elif c == 3:
                    pe.wait_ge(v_ok, RT * i + 1)
                elif before:
                    pe.wait_ge(u_ok, RT * (i - 3) + c + 1)
                elif isinstance(i, int) and i > 0:
                    if c == 0:
                        pe.wait_ge(v_ok, RT * i)
                    else:
                        pe.wait_ge(qk_lo_ok, NQ * i)
                if c == 0:
                    pe.wait_ge(xc_lo_ok, 2 * i + 2)
                cols = slice(P * c, P * c + P)
                for n, (hi, lo) in enumerate(((x_hi, x_lo), (c_hi, c_lo))):
                    for k in range(KT):
                        mm = three_passes(pe, pj_bank[c % 2][:, n * S:(n + 1) * S], wk_hi[:, k, cols],
                                          wk_lo[:, k, cols], hi[:, k], lo[:, k], k == 0, k == KT - 1)
                mm.then_inc(qk_mm, 1)

            def scores(i, c, heads):
                if 0 in heads:
                    pe.wait_ge(q_in[c % 2], 128 * i + 64 * (c // 2 + 1))
                for h in heads:
                    n = HQ * c + h
                    if n >= 2 or not (isinstance(i, int) and i == 0):
                        pe.wait_ge(s_ok, 16 * i + n - 1)
                    dst = s_bank[h % 2]
                    q_hi, q_lo = q_alone[:, c % 2, 0, h], q_alone[:, c % 2, 1, h]
                    k_hi, k_lo = qk_parts[:, c % 2, 2], qk_parts[:, c % 2, 3]
                    three_passes(pe, dst[:, 0:LATE], q_hi[:, P:S], q_lo[:, P:S], k_hi, k_lo, True, True)
                    three_passes(pe, dst[:, LATE:SPAN], q_hi[:, 0:P], q_lo[:, 0:P],
                                 k_hi[:, P:S], k_lo[:, P:S], True, True).then_inc(s_mm, 1)

            def transposes(i, c):
                for n in range(3 * HQ):
                    h, piece = n // 3, n % 3
                    if piece == 0:
                        pe.wait_ge(p_ok, 16 * i + HQ * c + h + 1)
                    if n % 4 == 0 and (c > 0 or not (isinstance(i, int) and i == 0)):
                        pe.wait_ge(pt_ok, 12 * i + 3 * (c - 1) + n // 4 + 1)
                    at = (LATE, P, 0)[piece]
                    mm = nc.tensor.transpose(pt_bank[n // 4][:, P * (n % 4):P * (n % 4) + P],
                                             p_sb[:, h, at:at + P], ident[:])
                    if n % 4 == 3:
                        mm.then_inc(pt_mm, 1)

            def attend_quad(i, slot, c):
                pe.wait_ge(pt_ok, 12 * i + 3 * c + 3)
                if c == 0:
                    pe.wait_ge(v_ok, RT * i + RT)
                if c > 0 or not (isinstance(i, int) and i == 0):
                    pe.wait_ge(cc_ok, NQ * i + c)
                pe.wait_ge(wide_ok, NQ * i + c + 1)
                for t in range(RT):
                    at = S + P * (1 - t)
                    nc.tensor.matmul(av_bank[:, at:at + P], zi_wide[:, t].rearrange("p h d -> p (h d)"),
                                          ident[:], start=True, stop=True, skip_group_check=True)
                for part in range(2):
                    for h in range(HQ):
                        feat = DK * (HQ * c + h)
                        rows = slice(DK * h, DK * h + DK)
                        lhs = v_sb[:, slot, 1 - part, feat:feat + DK]
                        if part == 0:
                            nc.tensor.matmul(av_bank[rows, 0:S], lhs, pt_sb[:, c % 2, h, 0:S],
                                             start=True, stop=False, skip_group_check=True)
                        else:
                            mm = nc.tensor.matmul(av_bank[rows, P:S], lhs, pt_sb[:, c % 2, h, S:SPAN],
                                             start=False, stop=True, skip_group_check=True)
                mm.then_inc(av_mm, 1)

            def step(i, slot, now, last, older, ahead, load):
                if now:
                    scores(i, 0, (2, 3))
                if older:
                    attend_quad(i - 2, slot, 3)
                if now:
                    queries_keys(i, 2, older)
                    values(i, 0)
                if last:
                    transposes(i - 1, 0)
                if now:
                    scores(i, 1, (0, 1))
                    values(i, 1)
                    scores(i, 1, (2, 3))
                    queries_keys(i, 3, older)
                if last:
                    attend_quad(i - 1, 1 - slot, 0)
                if older:
                    project_rows(i, 0, now)
                if last:
                    transposes(i - 1, 1)
                if now:
                    scores(i, 2, (0, 1))
                if older:
                    project_rows(i, 1, now)
                if now:
                    scores(i, 2, (2, 3))
                if last:
                    attend_quad(i - 1, 1 - slot, 1)
                if ahead:
                    queries_keys(i + 1, 0, older)
                if last:
                    transposes(i - 1, 2)
                if now:
                    scores(i, 3, (0, 1))
                    scores(i, 3, (2, 3))
                if last:
                    attend_quad(i - 1, 1 - slot, 2)
                    transposes(i - 1, 3)
                if ahead:
                    queries_keys(i + 1, 1, older)
                if ahead:
                    scores(i + 1, 0, (0, 1))

            pe.wait_ge(w_hi_ok, 3)
            pe.wait_ge(w_lo_ok, 3)
            pe.wait_ge(const_ok, CONSTS)
            queries_keys(0, 0, False)
            queries_keys(0, 1, False)
            scores(0, 0, (0, 1))
            over_batches(pe, step)

            def turn_rows(g, slot, ks, first):
                for k in ks:
                    if k == 0:
                        pe.wait_ge(x1_in[slot], group_bytes(g, slot))
                    if first and k < 2:
                        pe.wait_ge(x1_out, 16 * B)
                    else:
                        pe.wait_ge(xt_hi_ok, KT * g + k - 1)
                        pe.wait_ge(xt_lo_ok, KT * g + k - 1)
                    for t in range(GT):
                        mm = nc.tensor.transpose(xt_bank[k % 2][:, P * t:P * t + P],
                                                 x1[:, slot, t, P * k:P * k + P], ident[:])
                    mm.then_inc(xt_mm, 1)

            def hidden(g, f, first):
                if f == 0:
                    pe.wait_ge(xt_hi_ok, KT * g + KT)
                    pe.wait_ge(xt_lo_ok, KT * g + KT)
                if f >= 2 or not first:
                    pe.wait_ge(h_ok, FT * g + f - 1)
                if first:
                    pe.wait_ge(ffw_hi_ok, 2 * f + 2)
                    pe.wait_ge(ffw_lo_ok, 2 * f + 2)
                for k in range(KT):
                    mm = three_passes(pe, h_bank[f % 2][:], w1_hi[:, f, k], w1_lo[:, f, k],
                                      xt_hi[:, k], xt_lo[:, k], k == 0, k == KT - 1)
                mm.then_inc(h_mm, 1)

            def add_hidden(g, f, first):
                pe.wait_ge(h_hi_ok, FT * g + f + 1)
                pe.wait_ge(h_lo_ok, FT * g + f + 1)
                for t in range(GT):
                    if f == 0 and not first:
                        pe.wait_ge(y_ok, GT * (g - 1) + t + 1)
                    rows = slice(P * t, P * t + P)
                    mm = three_passes(pe, y_bank[t][:], h_hi[:, f % 2, rows], h_lo[:, f % 2, rows],
                                      w2_hi[:, f], w2_lo[:, f], f == 0, f == FT - 1)
                mm.then_inc(y_step, 1)

            def group(g, slot, first, last):
                for f in range(FT):
                    hidden(g, f, first)
                    if f == FT - 1 and not last:
                        turn_rows(g + 1, 1 - slot, (0, 1), False)
                    if f >= 1:
                        add_hidden(g, f - 1, first)
                if not last:
                    turn_rows(g + 1, 1 - slot, (2, 3), False)
                add_hidden(g, FT - 1, first)

            turn_rows(0, 0, range(KT), True)
            over_groups(pe, group)

        @block.scalar
        def _(act):
            act.wait_ge(gam_dve, 1)
            nc.scalar.activation(g_tmp[:, 1], g_tmp[:, 0], ACT.Exp).then_inc(gam_act, 1)
            act.wait_ge(const_ok, CONSTS)
            act.wait_ge(cons_in, 16 * 6)

            def qk_high(i, c):
                act.wait_ge(qk_mm, NQ * i + c + 1)
                if c >= 2:
                    act.wait_ge(s_mm, 16 * i + HQ * (c - 1))
                elif not (isinstance(i, int) and i == 0):
                    act.wait_ge(s_mm, 16 * (i - 1) + HQ * (c + 3))
                nc.scalar.activation(qk_parts[:, c % 2, 0:4:2], pj_bank[c % 2][:].rearrange("p (n s) -> p n s", n=2),
                                     ACT.Identity, bias=bk_col[:, c:c + 1]).then_inc(qk_hi_ok, 1)

            def first_exp(i, c, last):
                act.wait_ge(nm1_ok, NQ * i + c + 1)
                if last:
                    act.wait_ge(p_ok, 16 * (i - 1) + HQ * c + HQ)
                for h in range(HQ):
                    for late in (True, False):
                        a, z = head_block(c, h, late)
                        src = s_sb[:, c, h, 0:LATE] if late else s_sb[:, c, h, LATE:SPAN]
                        t = 0 if late else 1
                        e = nc.scalar.activation(w_sb[:, c, a + 1:z + 1], src, ACT.Exp, scale=SCALE,
                                                 bias=nm1[:, c, h, t:t + 1])
                e.then_inc(e1_ok, 1)

            def roots(i, quads):
                for c in quads:
                    act.wait_ge(r_ok, NQ * i + c + 1)
                    nc.scalar.activation(w_sb[:, c], w_sb[:, c], ACT.Sqrt, bias=tiny[:]).then_inc(root_ok, 1)

            def effect(i, c):
                act.wait_ge(root_ok, NQ * i + c + 1)
                nc.scalar.activation(w_sb[:, c], w_sb[:, c], ACT.Exp, scale=-1.0).then_inc(te_ok, 1)

            def second_exp(i, c):
                act.wait_ge(nm2_ok, NQ * i + c + 1)
                for h in range(HQ):
                    if c >= 1 or not (isinstance(i, int) and i == 0):
                        act.wait_ge(pt_mm, 12 * i + 3 * (c - 1) + (1, 2, 3, 3)[h])
                    for late in (True, False):
                        a, z = head_block(c, h, late)
                        dst = p_sb[:, h, 0:LATE] if late else p_sb[:, h, LATE:SPAN]
                        t = 0 if late else 1
                        e = nc.scalar.activation(dst, w_sb[:, c, a:z], ACT.Exp, scale=SCALE,
                                                 bias=nm2[:, c, h, t:t + 1], accum_out=z2[:, c, h, t:t + 1])
                    e.then_inc(p_ok, 1)

            def turned(i, c):
                flat = pt_sb[:, c % 2].rearrange("p h s -> p (h s)")
                for n in range(3):
                    act.wait_ge(pt_mm, 12 * i + 3 * c + n + 1)
                    if n == 0 and (c >= 2 or not (isinstance(i, int) and i == 0)):
                        act.wait_ge(av_mm, NQ * i + c - 1)
                    nc.scalar.copy(flat[:, 512 * n:512 * n + 512], pt_bank[n][:]).then_inc(pt_ok, 1)

            def reciprocals(i, c):
                act.wait_ge(av_mm, NQ * i + c + 1)
                if c >= 2 or not (isinstance(i, int) and i == 0):
                    act.wait_ge(cc_lo_ok, NQ * i + c - 1)
                nc.scalar.copy(cc_sb[:, c % 2], av_bank[:, S:2 * S]).then_inc(zi_row_ok, 1)

            def step(i, slot, now, last, older, ahead, load):
                for c in range(NQ):
                    if last:
                        second_exp(i - 1, c)
                    if c == 3 and ahead:
                        qk_high(i + 1, 0)
                    if c == 0 and older:
                        reciprocals(i - 2, 3)
                    if c == 1 and last:
                        roots(i - 1, (2, 3))
                    if c == 1 and now:
                        qk_high(i, 3)
                    if c == 1 and last:
                        effect(i - 1, 2)
                        effect(i - 1, 3)
                    if c == 3 and now:
                        roots(i, (0, 1))
                        effect(i, 0)
                        effect(i, 1)
                    if c > 0 and last:
                        reciprocals(i - 1, c - 1)
                    if c == 3 and ahead:
                        qk_high(i + 1, 1)
                    if now:
                        first_exp(i, c, last)
                    if c == 0 and now:
                        qk_high(i, 2)
                    if last:
                        turned(i - 1, c)

            qk_high(0, 0)
            qk_high(0, 1)
            over_batches(act, step)

            act.wait_ge(x1_out, 16 * B)
            act.wait_ge(ffc_in, 16 * 4)

            def rows_high(g, first):
                for k in range(KT):
                    act.wait_ge(xt_mm, KT * g + k + 1)
                    if k == 0 and not first:
                        act.wait_ge(h_mm, FT * g)
                    nc.scalar.copy(xt_hi[:, k], xt_bank[k % 2][:]).then_inc(xt_hi_ok, 1)

            def group(g, slot, first, last):
                for f in range(FT):
                    act.wait_ge(h_mm, FT * g + f + 1)
                    if f >= 2 or not first:
                        act.wait_ge(h_lo_ok, FT * g + f - 1)
                    nc.scalar.activation(h_sb[:, f % 2], h_bank[f % 2][:], ACT.Relu,
                                         bias=b1_col[:, f:f + 1]).then_inc(h_ok, 1)
                    act.wait_ge(h_ok, FT * g + f + 1)
                    if f >= 2 or not first:
                        act.wait_ge(y_step, FT * g + f - 1)
                    nc.scalar.copy(h_hi[:, f % 2], h_sb[:, f % 2]).then_inc(h_hi_ok, 1)
                if not last:
                    rows_high(g + 1, False)

            rows_high(0, True)
            over_groups(act, group)

        @block.vector
        def _(dve):
            for n, hi in enumerate((wk_hi, wv_hi, wo_hi)):
                dve.wait_ge(wraw_in, 16 * 3)
                nc.vector.tensor_copy(hi[:].rearrange("p k n -> p (k n)"),
                                      s_sb_flat(s_sb)[:, n * KT * D:(n + 1) * KT * D]).then_inc(w_hi_ok, 1)

            def split_inputs(i, done):
                dve.wait_ge(xraw_in, 16 * i + 16)
                dve.wait_ge(craw_in, 16 * i + 16)
                if done:
                    dve.wait_ge(qk_mm, NQ * i)
                    dve.wait_ge(v_mm, RT * i)
                nc.vector.tensor_copy(x_hi[:], x_raw[:]).then_inc(xc_hi_ok, 1)
                nc.vector.tensor_copy(c_hi[:], c_raw[:]).then_inc(xc_hi_ok, 1)

            split_inputs(0, False)
            dve.wait_ge(cons_in, 16 * 6)
            chain = [0]

            def then(ins):
                chain[0] += 1
                ins.then_inc(gam_dve, 1)
                dve.wait_ge(gam_dve, chain[0])

            minus_abs, y, two_y, inv, z, zz, acc, sp = (g_tmp[:, n] for n in range(8))
            then(nc.vector.scalar_tensor_tensor(minus_abs, g_in[:], -1.0, g_in[:], ALU.mult, ALU.min))
            dve.wait_ge(gam_act, 1)
            then(nc.vector.tensor_scalar(two_y, y, 2.0, None, ALU.add))
            then(nc.vector.reciprocal(inv, two_y))
            then(nc.vector.tensor_tensor(z, y, inv, ALU.mult))
            then(nc.vector.tensor_tensor(zz, z, z, ALU.mult))
            then(nc.vector.tensor_scalar(acc, zz, 1.0 / 15, None, ALU.mult))
            for n in range(13, 1, -2):
                then(nc.vector.scalar_tensor_tensor(acc, acc, 1.0 / n, zz, ALU.add, ALU.mult))
            then(nc.vector.scalar_tensor_tensor(acc, acc, 1.0, z, ALU.add, ALU.mult))
            then(nc.vector.tensor_scalar(acc, acc, 2.0, None, ALU.mult))
            then(nc.vector.scalar_tensor_tensor(sp, g_in[:], 0.0, acc, ALU.max, ALU.add))
            for t in range(2):
                then(nc.vector.tensor_tensor(gamma2[:, :, t], sp, sp, ALU.mult))
            dve.wait_ge(const_ok, CONSTS)
            dve.wait_ge(w_lo_ok, 3)

            def qk_low(i, c):
                dve.wait_ge(qk_hi_ok, NQ * i + c + 1)
                src = pj_bank[c % 2][:].rearrange("p (n s) -> p n s", n=2)
                nc.vector.scalar_tensor_tensor(qk_parts[:, c % 2, 1:4:2], src, bk_col[:, c:c + 1],
                                               qk_parts[:, c % 2, 0:4:2].bitcast(F32), ALU.add,
                                               ALU.subtract).then_inc(qk_lo_ok, 1)

            def value_rows(i, slot, t, older):
                if older and t == 0:
                    dve.wait_ge(av_mm, NQ * (i - 2) + NQ)
                dve.wait_ge(v_mm, RT * i + t + 1)
                nc.vector.tensor_tensor(v_sb[:, slot, t], pj_bank[1 - t][:], bv_bc[:], ALU.add).then_inc(v_ok, 1)

            def mask_scores(i, c, heads):
                for h in heads:
                    dve.wait_ge(s_mm, 16 * i + HQ * c + h + 1)
                    alone(dve)
                    nc.vector.tensor_tensor_reduce(
                        out=s_sb[:, c, h, 0:LATE], in0=s_bank[h % 2][:, 0:LATE], in1=mask[:],
                        scale=1.0, scalar=NEG, op0=ALU.add, op1=ALU.max, accum_out=m1[:, c, h, 0:1])
                    nc.vector.tensor_tensor_reduce(
                        out=s_sb[:, c, h, LATE:SPAN], in0=s_bank[h % 2][:, LATE:SPAN], in1=mask[:, 0:EARLY],
                        scale=1.0, scalar=NEG, op0=ALU.add, op1=ALU.max,
                        accum_out=m1[:, c, h, 1:2]).then_inc(s_ok, 1)
                if HQ - 1 in heads:
                    dve.wait_ge(s_ok, 16 * i + HQ * c + HQ)
                    nc.vector.tensor_scalar(nm1[:, c], m1[:, c], -SCALE, None, ALU.mult).then_inc(nm1_ok, 1)

            def running_sums(i, c):
                dve.wait_ge(e1_ok, NQ * i + c + 1)
                blocks = w_sb[:, c].rearrange("p (h w) -> p h w", h=HQ)
                nc.vector.memset(blocks[:, :, 0:LATE + 2:LATE + 1], 0.0).then_inc(zero_ok, 1)
                dve.wait_ge(zero_ok, NQ * i + c + 1)
                nc.vector.tensor_tensor_scan(w_sb[:, c], carry[:], w_sb[:, c], 0.0,
                                             ALU.mult, ALU.add).then_inc(scan_ok, 1)
                dve.wait_ge(scan_ok, NQ * i + c + 1)
                nc.vector.reciprocal(zi[:, c], blocks[:, :, LATE:BLK:EARLY + 1]).then_inc(zi_ok, 1)
                dve.wait_ge(zi_ok, NQ * i + c + 1)
                nc.vector.tensor_tensor(gz[:, c], zi[:, c], gamma2[:, HQ * c:HQ * c + HQ],
                                        ALU.mult).then_inc(gz_ok, 1)

            def decay(i, c):
                dve.wait_ge(t_ok, NQ * i + c + 1)
                dve.wait_ge(gz_ok, NQ * i + c + 1)
                for h in range(HQ):
                    for t in range(2):
                        a, z = head_block(c, h, t == 0)
                        r = nc.vector.tensor_scalar(w_sb[:, c, a:z], w_sb[:, c, a:z], gz[:, c, h, t:t + 1],
                                                    R_MAX, ALU.mult, ALU.min)
                r.then_inc(r_ok, 1)

            def decayed_scores(i, c):
                dve.wait_ge(te_ok, NQ * i + c + 1)
                alone(dve)
                for h in range(HQ):
                    for t in range(2):
                        a, z = head_block(c, h, t == 0)
                        src = s_sb[:, c, h, 0:LATE] if t == 0 else s_sb[:, c, h, LATE:SPAN]
                        r = nc.vector.tensor_tensor_reduce(
                            out=w_sb[:, c, a:z], in0=w_sb[:, c, a:z], in1=src, scale=1.0, scalar=NEG,
                            op0=ALU.mult, op1=ALU.max, accum_out=m2[:, c, h, t:t + 1])
                r.then_inc(s2_ok, 1)
                dve.wait_ge(s2_ok, NQ * i + c + 1)
                nc.vector.tensor_scalar(nm2[:, c], m2[:, c], -SCALE, None, ALU.mult).then_inc(nm2_ok, 1)

            def totals(i, c):
                dve.wait_ge(p_ok, 16 * i + HQ * c + HQ)
                nc.vector.reciprocal(z2[:, c], z2[:, c]).then_inc(zi2_ok, 1)
                dve.wait_ge(zi2_ok, NQ * i + c + 1)
                if c > 0 or not (isinstance(i, int) and i == 0):
                    dve.wait_ge(av_mm, NQ * i + c)
                nc.vector.tensor_copy(zi_wide[:].rearrange("p t h d -> p h t d"),
                                      z2[:, c].unsqueeze(3).broadcast_to([P, HQ, 2, DK])).then_inc(wide_ok, 1)

            def concat(i, c):
                dve.wait_ge(zi_row_ok, NQ * i + c + 1)
                nc.vector.tensor_tensor(cc_sb[:, c % 2], av_bank[:, 0:S], cc_sb[:, c % 2], ALU.mult).then_inc(cc_ok, 1)

            def residual(i, t):
                dve.wait_ge(xb_ok, i + 1)
                if t == 0 and not (isinstance(i, int) and i == 0):
                    dve.wait_ge(x1_out, 16 * i)
                dve.wait_ge(wo_mm, RT * i + t + 1)
                nc.vector.tensor_tensor(u_sb[:, t], pj_bank[t][:], xrow[:, t], ALU.add).then_inc(u_ok, 1)

            def moments(i):
                for t in range(RT):
                    dve.wait_ge(u_ok, RT * i + t + 1)
                    nc.vector.bn_stats(bn1[:, t], u_sb[:, t]).then_inc(bn1_ok, 1)
                for t in range(RT):
                    dve.wait_ge(bn1_ok, RT * i + t + 1)
                    alone(dve)
                    nc.vector.bn_aggr(mv1[:, t], bn1[:, t]).then_inc(mv1_ok, 1)

            def normalise(i):
                dve.wait_ge(rstd1_ok, i + 1)
                for t in range(RT):
                    nc.vector.tensor_scalar(u_sb[:, t], u_sb[:, t], mv1[:, t, 0:1], rstd1[:, t:t + 1],
                                            ALU.subtract, ALU.mult).then_inc(norm1_ok, 1)

            def step(i, slot, now, last, older, ahead, load):
                if now:
                    mask_scores(i, 0, (0, 1))
                if older:
                    concat(i - 2, 2)
                if now:
                    mask_scores(i, 0, (2, 3))
                    qk_low(i, 1)
                if last:
                    running_sums(i - 1, 3)
                    decayed_scores(i - 1, 1)
                if now:
                    qk_low(i, 2)
                if older:
                    concat(i - 2, 3)
                if now:
                    value_rows(i, slot, 0, older)
                if last:
                    decay(i - 1, 3)
                    totals(i - 1, 0)
                if now:
                    mask_scores(i, 1, range(HQ))
                    value_rows(i, slot, 1, older)
                    running_sums(i, 0)
                    qk_low(i, 3)
                if older:
                    residual(i - 2, 0)
                if ahead:
                    split_inputs(i + 1, True)
                if last:
                    concat(i - 1, 0)
                if now:
                    decay(i, 0)
                if last:
                    decayed_scores(i - 1, 2)
                if now:
                    mask_scores(i, 2, (0, 1))
                if last:
                    totals(i - 1, 1)
                if older:
                    residual(i - 2, 1)
                if now:
                    mask_scores(i, 2, (2, 3))
                    running_sums(i, 1)
                if last:
                    decayed_scores(i - 1, 3)
                    concat(i - 1, 1)
                if now:
                    decay(i, 1)
                if last:
                    totals(i - 1, 2)
                if now:
                    mask_scores(i, 3, range(HQ))
                if ahead:
                    qk_low(i + 1, 0)
                if now:
                    running_sums(i, 2)
                if older:
                    moments(i - 2)
                if last:
                    totals(i - 1, 3)
                if now:
                    decay(i, 2)
                if older:
                    normalise(i - 2)
                if now:
                    decayed_scores(i, 0)

            qk_low(0, 0)
            over_batches(dve, step)

            dve.wait_ge(x1_out, 16 * B)
            dve.wait_ge(ffc_in, 16 * 4)

            def weights_high(f):
                dve.wait_ge(ffw_in[f % 2], 32 * (f // 2 + 1))
                nc.vector.tensor_copy(w1_hi[:, f].rearrange("p k m -> p (k m)"), w_raw[:, f % 2, 0]).then_inc(ffw_hi_ok, 1)
                nc.vector.tensor_copy(w2_hi[:, f], w_raw[:, f % 2, 1]).then_inc(ffw_hi_ok, 1)

            def rows_low(g):
                for k in range(KT):
                    dve.wait_ge(xt_hi_ok, KT * g + k + 1)
                    nc.vector.tensor_tensor(xt_lo[:, k], xt_bank[k % 2][:], xt_hi[:, k].bitcast(F32),
                                            ALU.subtract).then_inc(xt_lo_ok, 1)

            def group_moments(g):
                for t in range(GT):
                    dve.wait_ge(y_ok, GT * g + t + 1)
                    nc.vector.bn_stats(bn2[:, t], y_sb[:, t]).then_inc(bn2_ok, 1)
                for t in range(GT):
                    dve.wait_ge(bn2_ok, GT * g + t + 1)
                    alone(dve)
                    nc.vector.bn_aggr(mv2[:, t], bn2[:, t]).then_inc(mv2_ok, 1)

            def group_normalise(g):
                dve.wait_ge(rstd2_ok, g + 1)
                for t in range(GT):
                    nc.vector.tensor_scalar(y_sb[:, t], y_sb[:, t], mv2[:, t, 0:1], rstd2[:, t:t + 1],
                                            ALU.subtract, ALU.mult).then_inc(norm2_ok, 1)

            def group(g, slot, first, last):
                for f in range(FT):
                    if first and f + 2 < FT:
                        weights_high(f + 2)
                    dve.wait_ge(h_hi_ok, FT * g + f + 1)
                    nc.vector.tensor_tensor(h_lo[:, f % 2], h_sb[:, f % 2], h_hi[:, f % 2].bitcast(F32),
                                            ALU.subtract).then_inc(h_lo_ok, 1)
                    if f == 1 and not first:
                        group_moments(g - 1)
                    if f == 3 and not first:
                        group_normalise(g - 1)
                if not last:
                    rows_low(g + 1)
                dve.wait_ge(y_step, FT * g + FT)
                dve.wait_ge(xb2_ok, g + 1)
                if not first:
                    dve.wait_ge(out_st, 16 * g)
                for t in range(GT):
                    nc.vector.tensor_tensor(y_sb[:, t], y_bank[t][:], x1[:, slot, t], ALU.add).then_inc(y_ok, 1)
                if last:
                    group_moments(g)
                    group_normalise(g)

            weights_high(0)
            weights_high(1)
            rows_low(0)
            over_groups(dve, group)

        @block.gpsimd
        def _(pool):
            nc.gpsimd.iota(iota_i, pattern=[[1, S]], base=1 - P, channel_multiplier=1).then_inc(const_ok, 1)
            nc.gpsimd.memset(mask[:], 0.0).then_inc(const_ok, 1)
            nc.gpsimd.memset(ident[:], 0.0).then_inc(const_ok, 1)
            nc.gpsimd.memset(carry[:], 1.0).then_inc(const_ok, 1)
            nc.gpsimd.memset(half[:], -0.5).then_inc(const_ok, 1)
            nc.gpsimd.memset(tiny[:], R_TINY).then_inc(const_ok, 1)
            nc.gpsimd.memset(q_alone[:].bitcast(F32), 0.0).then_inc(const_ok, 1)
            pool.wait_ge(const_ok, 7)
            nc.gpsimd.tensor_copy(dist[:], iota_i).then_inc(const_ok, 1)
            nc.gpsimd.affine_select(out=mask[:], in_=mask[:], compare_op=ALU.is_ge, fill=NEG, base=1 - P,
                                    pattern=[[1, S]], channel_multiplier=1).then_inc(const_ok, 1)
            nc.gpsimd.affine_select(out=ident[:], in_=ident[:], compare_op=ALU.not_equal, fill=1.0, base=0,
                                    pattern=[[-1, P]], channel_multiplier=1).then_inc(const_ok, 1)
            nc.gpsimd.memset(carry[:].rearrange("p (h w) -> p h w", h=HQ)[:, :, 0:LATE + 2:LATE + 1],
                             0.0).then_inc(const_ok, 1)
            for n, (hi, lo) in enumerate(((wk_hi, wk_lo), (wv_hi, wv_lo), (wo_hi, wo_lo))):
                pool.wait_ge(w_hi_ok, n + 1)
                nc.gpsimd.tensor_tensor(lo[:].rearrange("p k n -> p (k n)"),
                                        s_sb_flat(s_sb)[:, n * KT * D:(n + 1) * KT * D],
                                        hi[:].rearrange("p k n -> p (k n)").bitcast(F32),
                                        ALU.subtract).then_inc(w_lo_ok, 1)

            def split_inputs(i):
                for n, (raw, hi, lo) in enumerate(((x_raw, x_hi, x_lo), (c_raw, c_hi, c_lo))):
                    pool.wait_ge(xc_hi_ok, 2 * i + n + 1)
                    nc.gpsimd.tensor_tensor(lo[:], raw[:], hi[:].bitcast(F32), ALU.subtract).then_inc(xc_lo_ok, 1)

            split_inputs(0)
            pool.wait_ge(const_ok, CONSTS)
            pool.wait_ge(cons_in, 16 * 6)

            def add_bias(i):
                pool.wait_ge(xrow_in, 16 * i + 16)
                nc.gpsimd.tensor_tensor(xrow[:], xrow[:], bo_bc[:].unsqueeze(1).broadcast_to([P, RT, D]),
                                        ALU.add).then_inc(xb_ok, 1)

            def times_distance(i, c):
                pool.wait_ge(scan_ok, NQ * i + c + 1)
                blocks = w_sb[:, c].rearrange("p (h w) -> p h w", h=HQ)
                nc.gpsimd.tensor_tensor(blocks[:, :, 0:LATE], blocks[:, :, 0:LATE],
                                        dist[:].unsqueeze(1).broadcast_to([P, HQ, LATE]), ALU.mult)
                nc.gpsimd.tensor_tensor(blocks[:, :, LATE + 1:BLK - 1], blocks[:, :, LATE + 1:BLK - 1],
                                        dist[:, 0:EARLY].unsqueeze(1).broadcast_to([P, HQ, EARLY]),
                                        ALU.mult).then_inc(t_ok, 1)

            def split_concat(i, c):
                pool.wait_ge(cc_ok, NQ * i + c + 1)
                if c == 0 and not (isinstance(i, int) and i == 0):
                    pool.wait_ge(wo_mm, RT * i)
                alone(pool)
                nc.gpsimd.tensor_copy(cc_hi[:, c], cc_sb[:, c % 2]).then_inc(cc_hi_ok, 1)
                pool.wait_ge(cc_hi_ok, NQ * i + c + 1)
                nc.gpsimd.tensor_tensor(cc_lo[:, c], cc_sb[:, c % 2], cc_hi[:, c].bitcast(F32),
                                        ALU.subtract).then_inc(cc_lo_ok, 1)

            def deviation(i):
                pool.wait_ge(mv1_ok, RT * i + RT)
                alone(pool)
                nc.gpsimd.tensor_scalar(rstd1[:], mv1[:, :, 1], EPS_LN, None, ALU.add).then_inc(ve1_ok, 1)
                pool.wait_ge(ve1_ok, i + 1)
                nc.gpsimd.tensor_tensor(rstd1[:], rstd1[:], half[:, 0:RT], ALU.pow).then_inc(rstd1_ok, 1)

            def scale_shift(i):
                pool.wait_ge(norm1_ok, RT * i + RT)
                nc.gpsimd.tensor_tensor(u_sb[:], u_sb[:], l1w_bc[:].unsqueeze(1).broadcast_to([P, RT, D]),
                                        ALU.mult).then_inc(scaled1_ok, 1)
                pool.wait_ge(scaled1_ok, i + 1)
                nc.gpsimd.tensor_tensor(u_sb[:], u_sb[:], l1b_bc[:].unsqueeze(1).broadcast_to([P, RT, D]),
                                        ALU.add).then_inc(x1_ok, 1)

            def step(i, slot, now, last, older, ahead, load):
                if last:
                    times_distance(i - 1, 3)
                if older:
                    split_concat(i - 2, 2)
                    split_concat(i - 2, 3)
                    add_bias(i - 2)
                if now:
                    times_distance(i, 0)
                if last:
                    split_concat(i - 1, 0)
                if ahead:
                    split_inputs(i + 1)
                if now:
                    times_distance(i, 1)
                if last:
                    split_concat(i - 1, 1)
                if now:
                    times_distance(i, 2)
                if older:
                    deviation(i - 2)
                    scale_shift(i - 2)

            over_batches(pool, step)

            pool.wait_ge(x1_out, 16 * B)
            pool.wait_ge(ffc_in, 16 * 4)

            def weights_low(f):
                pool.wait_ge(ffw_hi_ok, 2 * f + 2)
                nc.gpsimd.tensor_tensor(w1_lo[:, f].rearrange("p k m -> p (k m)"), w_raw[:, f % 2, 0],
                                        w1_hi[:, f].rearrange("p k m -> p (k m)").bitcast(F32),
                                        ALU.subtract).then_inc(ffw_lo_ok, 1)
                nc.gpsimd.tensor_tensor(w2_lo[:, f], w_raw[:, f % 2, 1], w2_hi[:, f].bitcast(F32),
                                        ALU.subtract).then_inc(ffw_lo_ok, 1)

            def group_norm(g):
                pool.wait_ge(mv2_ok, GT * g + GT)
                alone(pool)
                nc.gpsimd.tensor_scalar(rstd2[:], mv2[:, :, 1], EPS_LN, None, ALU.add).then_inc(ve2_ok, 1)
                pool.wait_ge(ve2_ok, g + 1)
                nc.gpsimd.tensor_tensor(rstd2[:], rstd2[:], half[:], ALU.pow).then_inc(rstd2_ok, 1)
                for t in range(GT):
                    pool.wait_ge(norm2_ok, GT * g + t + 1)
                    nc.gpsimd.tensor_tensor(y_sb[:, t], y_sb[:, t], l2w_bc[:], ALU.mult).then_inc(scaled2_ok, 1)
                    pool.wait_ge(scaled2_ok, GT * g + t + 1)
                    nc.gpsimd.tensor_tensor(y_sb[:, t], y_sb[:, t], l2b_bc[:], ALU.add).then_inc(out_ok, 1)

            def group(g, slot, first, last):
                if first:
                    for f in range(2, FT):
                        weights_low(f)
                else:
                    group_norm(g - 1)
                pool.wait_ge(xt_mm, KT * g + KT)
                nc.gpsimd.tensor_tensor(x1[:, slot], x1[:, slot], b2_bc[:].unsqueeze(1).broadcast_to([P, GT, D]),
                                        ALU.add).then_inc(xb2_ok, 1)
                if last:
                    group_norm(g)

            weights_low(0)
            weights_low(1)
            over_groups(pool, group)


CONSTS = 11


def s_sb_flat(s_sb):
    return s_sb[:].rearrange("p c h w -> p (c h w)")


def group_bytes(g, slot):
    return 16 * (g // 2 + 1) if isinstance(g, int) else 8 * (g - slot) + 16


def kernel(**inputs):
    import numpy as np
    import concourse.bacc as bacc
    from concourse.bass_utils import run_bass_kernel_spmd

    a = {k.removeprefix("L0_xattn_"): np.asarray(v) for k, v in inputs.items()}
    x, ctx = a["x"], a["ctx_1024"]
    B, S, D = x.shape
    F = a["b1"].shape[0]
    kt, ft = D // P, F // P

    def features_first(t):
        return t.reshape(B, S, kt, P).transpose(0, 3, 2, 1)

    def weight(w):
        return w.reshape(w.shape[0], w.shape[1] // P, P).transpose(2, 1, 0)

    arrays = {
        "x_rows": x, "x_t": features_first(x), "ctx_t": features_first(ctx[:, ::-1]),
        "wk": weight(a["Wk"]), "bk": a["bk"].reshape(kt, P).transpose(1, 0),
        "wv": weight(a["Wv"]), "bv": a["bv"], "wo": weight(a["Wo"]), "bo": a["bo"],
        "gammas": a["gammas"].reshape(-1), "ln1_w": a["ln1_w"], "ln1_b": a["ln1_b"],
        "w1": a["W1"].reshape(ft, P, kt, P).transpose(3, 0, 2, 1), "b1": a["b1"].reshape(ft, P).transpose(1, 0),
        "w2": weight(a["W2"]), "b2": a["b2"], "ln2_w": a["ln2_w"], "ln2_b": a["ln2_b"],
    }
    arrays = {k: np.ascontiguousarray(v) for k, v in arrays.items()}
    nc = bacc.Bacc("TRN2", target_bir_lowering=False, num_devices=1)
    aps = [nc.dram_tensor(k, v.shape, mybir.dt.from_np(v.dtype), kind="ExternalInput").ap()
           for k, v in arrays.items()]
    out = nc.dram_tensor("out", (B, S, D), F32, kind="ExternalOutput").ap()
    build(nc, *aps, out)
    r = run_bass_kernel_spmd(nc, [arrays], core_ids=[0])
    return r.results[0]["out"]
```

```python
from contextlib import ExitStack

import concourse.bass as bass
from concourse import mybir

F32 = mybir.dt.float32
F32R = mybir.dt.float32r
I32 = mybir.dt.int32
ALU = mybir.AluOpType
ACT = mybir.ActivationFunctionType
AX_X = mybir.AxisListType.X

P = 128
NEG = -1e32
EPS_LN = 1e-5
R_MAX = 132.54745276195996
R_TINY = 1e-30


def build(nc, x_rows, x_t, ctx_t, wk, bk, wv, bv, wo, bo, gammas, ln1_w, ln1_b,
          w1, b1, w2, b2, ln2_w, ln2_b, out):
    B, S, D = x_rows.shape
    H = gammas.shape[0]
    F = b1.shape[1] * P
    DK = D // H
    KT = D // P
    RT = S // P
    NQ = D // P
    HQ = P // DK
    FT = F // P
    SCALE = 1.0 / float(DK) ** 0.5
    assert RT == 2 and HQ == 4 and NQ == 4
    LATE, EARLY = S, P
    SPAN = LATE + EARLY
    BLK = SPAN + 2
    QW = HQ * BLK
    GR = 512
    GT = GR // P
    NG = B * S // GR

    x1_dram = nc.dram_tensor("x1_rows", (B * S, D), F32, kind="Internal").ap()
    x1_by_batch = x1_dram.rearrange("(b t p) n -> b p t n", b=B, p=P)
    x1_by_group = x1_dram.rearrange("(g t p) n -> g p t n", g=NG, p=P)
    x_by_batch = x_rows.rearrange("b (t p) n -> b p t n", p=P)
    out_by_group = out.rearrange("b s n -> (b s) n").rearrange("(g t p) n -> g p t n", g=NG, p=P)

    with ExitStack() as whole:
        def sem(name):
            return whole.enter_context(nc.semaphore(name))

        def tensor(stack, name, shape, dt=F32):
            return stack.enter_context(nc.sbuf_tensor(name, shape, dt))

        bank = [whole.enter_context(nc.psum_tensor(f"bank{i}", [P, 512], F32)) for i in range(8)]

        ident = tensor(whole, "ident", [P, P])
        half = tensor(whole, "minus_half", [P, GT])
        tiny = tensor(whole, "tiny", [P, 1])

        ph1 = ExitStack()
        wk_hi, wk_lo, wv_hi, wv_lo = (tensor(ph1, n, [P, KT, D], F32R) for n in ("wk_hi", "wk_lo", "wv_hi", "wv_lo"))
        x_raw = tensor(ph1, "x_raw", [P, KT, S])
        c_raw = tensor(ph1, "c_raw", [P, KT, S])
        x_hi, x_lo, c_hi, c_lo = (tensor(ph1, n, [P, KT, S], F32R) for n in ("x_hi", "x_lo", "c_hi", "c_lo"))
        qk_parts = tensor(ph1, "qk_parts", [P, 2, 4, S], F32R)
        q_alone = tensor(ph1, "q_alone", [P, 2, 2, HQ, S], F32R)
        mask = tensor(ph1, "mask", [P, S])
        dist = tensor(ph1, "dist", [P, S])
        carry = tensor(ph1, "carry", [P, QW])
        bv_bc = tensor(ph1, "bv_bc", [P, D])
        s_sb = tensor(ph1, "s_sb", [P, NQ, HQ, SPAN])
        w_sb = tensor(ph1, "w_sb", [P, NQ, QW])
        wo_hi, wo_lo = (tensor(ph1, n, [P, KT, D], F32R) for n in ("wo_hi", "wo_lo"))
        v_sb = tensor(ph1, "v_sb", [P, 2, RT, D])
        p_sb = tensor(ph1, "p_sb", [P, HQ, SPAN])
        pt_sb = tensor(ph1, "pt_sb", [P, 2, HQ, SPAN])
        zi_wide = tensor(ph1, "zi_wide", [P, 2, HQ, DK])
        cc_sb = tensor(ph1, "cc_sb", [P, 2, S])
        cc_hi = tensor(ph1, "cc_hi", [P, NQ, S], F32R)
        cc_lo = tensor(ph1, "cc_lo", [P, NQ, S], F32R)
        xrow = tensor(ph1, "xrow", [P, RT, D])
        u_sb = tensor(ph1, "u_sb", [P, RT, D])
        bo_bc, l1w_bc, l1b_bc = (tensor(ph1, n, [P, D]) for n in ("bo_bc", "l1w_bc", "l1b_bc"))
        bk_col = tensor(ph1, "bk_col", [P, NQ])
        g_in = tensor(ph1, "g_in", [P, H])
        gamma2 = tensor(ph1, "gamma2", [P, H, 2])
        m1, nm1, zi, gz, m2, nm2, z2 = (
            tensor(ph1, n, [P, NQ, HQ, 2]) for n in ("m1", "nm1", "zi", "gz", "m2", "nm2", "z2"))
        bn1 = tensor(ph1, "bn1", [P, RT, 6])
        mv1 = tensor(ph1, "mv1", [P, RT, 2])
        rstd1 = tensor(ph1, "rstd1", [P, RT])
        iota_i = cc_sb[:, 0].bitcast(I32)
        g_tmp = cc_sb[:, 1, 0:8 * H].rearrange("p (n h) -> p n h", n=8)
        ph1.close()

        w_raw = tensor(whole, "w_raw", [P, 2, 2, 512])
        x1 = tensor(whole, "x1", [P, 2, GT, D])
        xt_hi, xt_lo = (tensor(whole, n, [P, KT, GR], F32R) for n in ("xt_hi", "xt_lo"))
        h_sb = tensor(whole, "h_sb", [P, 2, GR])
        h_hi, h_lo = (tensor(whole, n, [P, 2, GR], F32R) for n in ("h_hi", "h_lo"))
        b2_bc, l2w_bc, l2b_bc = (tensor(whole, n, [P, D]) for n in ("b2_bc", "l2w_bc", "l2b_bc"))
        b1_col = tensor(whole, "b1_col", [P, FT])
        bn2 = tensor(whole, "bn2", [P, GT, 6])
        mv2 = tensor(whole, "mv2", [P, GT, 2])
        rstd2 = tensor(whole, "rstd2", [P, GT])
        ffw = tensor(whole, "ffw", [P, FT, 4, 512], F32R)
        y_sb = tensor(whole, "y_sb", [P, GT, D])
        EARLY_TILES = 8

        wraw_in = [sem(f"{n}_raw_in") for n in ("wk", "wv", "wo")]
        col_in = sem("col_in")
        cons_in = sem("cons_in")
        const_ok = sem("const_ok")
        w_hi_ok = sem("w_hi_ok")
        wk_lo_ok = sem("wk_lo_ok")
        w_lo_ok = sem("w_lo_ok")
        gam_act = sem("gam_act")
        gam_dve = sem("gam_dve")
        xraw_in = sem("xraw_in")
        craw_in = sem("craw_in")
        xrow_in = sem("xrow_in")
        xc_hi_ok = sem("xc_hi_ok")
        xc_lo_ok = sem("xc_lo_ok")
        qk_mm = sem("qk_mm")
        v_mm = sem("v_mm")
        wo_mm = sem("wo_mm")
        qk_hi_ok = sem("qk_hi_ok")
        qk_lo_ok = sem("qk_lo_ok")
        q_in = [sem(f"q_in{n}") for n in range(2)]
        v_ok = sem("v_ok")
        s_mm = sem("s_mm")
        s_ok = sem("s_ok")
        nm1_ok = sem("nm1_ok")
        e1_ok = sem("e1_ok")
        zero_ok = sem("zero_ok")
        shifted_ok = sem("shifted_ok")
        scan_ok = sem("scan_ok")
        zi_ok = sem("zi_ok")
        gz_ok = sem("gz_ok")
        t_ok = sem("t_ok")
        r_ok = sem("r_ok")
        root_ok = sem("root_ok")
        te_ok = sem("te_ok")
        s2_ok = sem("s2_ok")
        nm2_ok = sem("nm2_ok")
        p_ok = sem("p_ok")
        pt_mm = sem("pt_mm")
        pt_ok = sem("pt_ok")
        av_mm = sem("av_mm")
        zi2_ok = sem("zi2_ok")
        wide_ok = sem("wide_ok")
        zi_row_ok = sem("zi_row_ok")
        cc_ok = sem("cc_ok")
        cc_hi_ok = sem("cc_hi_ok")
        cc_lo_ok = sem("cc_lo_ok")
        xb_ok = sem("xb_ok")
        u_ok = sem("u_ok")
        bn1_ok = sem("bn1_ok")
        mv1_ok = sem("mv1_ok")
        ve1_ok = sem("ve1_ok")
        rstd1_ok = sem("rstd1_ok")
        norm1_ok = sem("norm1_ok")
        scaled1_ok = sem("scaled1_ok")
        x1_ok = sem("x1_ok")
        x1_out = sem("x1_out")

        ffw_in = [sem(f"ffw_in{n}") for n in range(2)]
        ffw_hi_ok = sem("ffw_hi_ok")
        ffw_lo_ok = sem("ffw_lo_ok")
        ffc_in = sem("ffc_in")
        x1_in = [sem(f"x1_in{n}") for n in range(2)]
        xt_mm = sem("xt_mm")
        xt_hi_ok = sem("xt_hi_ok")
        xt_lo_ok = sem("xt_lo_ok")
        h_mm = sem("h_mm")
        h_ok = sem("h_ok")
        h_hi_ok = sem("h_hi_ok")
        h_lo_ok = sem("h_lo_ok")
        y_step = sem("y_step")
        xb2_ok = sem("xb2_ok")
        y_ok = sem("y_ok")
        bn2_ok = sem("bn2_ok")
        mv2_ok = sem("mv2_ok")
        ve2_ok = sem("ve2_ok")
        rstd2_ok = sem("rstd2_ok")
        norm2_ok = sem("norm2_ok")
        scaled2_ok = sem("scaled2_ok")
        out_ok = sem("out_ok")
        scaled_last_ok = sem("scaled_last_ok")
        out_last_ok = sem("out_last_ok")
        out_st = sem("out_st")

        s_bank, pt_bank, av_bank, pj_bank = bank[0:2], bank[2:5], bank[5], bank[6:8]
        y_bank, h_bank, xt_bank = bank[0:4], bank[4:6], bank[6:8]

        def head_block(c, h, late):
            at = h * BLK + (0 if late else LATE + 1)
            return at, at + (LATE if late else EARLY)

        def three_passes(pe, dst, a_hi, a_lo, b_hi, b_lo, start, stop):
            nc.tensor.matmul(dst, a_hi, b_hi, start=start, stop=False)
            nc.tensor.matmul(dst, a_hi, b_lo, start=False, stop=False)
            return nc.tensor.matmul(dst, a_lo, b_hi, start=False, stop=stop)

        def over_batches(engine, step):
            step(0, 0, True, False, False, True, True)
            step(1, 1, True, True, False, True, True)
            with engine.Fori(1, B // 2 - 1) as j:
                step(j * 2, 0, True, True, True, True, True)
                step(j * 2 + 1, 1, True, True, True, True, True)
            step(B - 2, 0, True, True, True, True, False)
            step(B - 1, 1, True, True, True, False, False)
            step(B, 0, False, True, True, False, False)
            step(B + 1, 1, False, False, True, False, False)

        def over_groups(engine, group):
            group(0, 0, True, False)
            with engine.Fori(1, NG // 2) as j:
                group(j * 2 - 1, 1, False, False)
                group(j * 2, 0, False, False)
            group(NG - 1, 1, False, True)

        carried = sem("carried")

        def alone(engine):
            engine.sem_inc(carried)

        block = whole.enter_context(nc.Block())

        @block.sync
        def _(sp):
            def raw_weight(n, w):
                sp.dma_start(s_sb_flat(s_sb)[:, n * KT * D:(n + 1) * KT * D],
                             w.rearrange("p k n -> p (k n)")).then_inc(wraw_in[n], 16)

            sp.sem_inc(x1_out)
            raw_weight(0, wk)
            sp.dma_start(x_raw[:], x_t[0]).then_inc(xraw_in, 16)
            sp.dma_start(c_raw[:], ctx_t[0]).then_inc(craw_in, 16)
            sp.dma_start(bk_col[:], bk).then_inc(col_in, 16)
            sp.dma_start(g_in[:], gammas.partition_broadcast(P)).then_inc(col_in, 16)
            raw_weight(1, wv)
            sp.dma_start(bv_bc[:], bv.partition_broadcast(P)).then_inc(cons_in, 16)
            raw_weight(2, wo)
            for dst, src in ((bo_bc, bo), (l1w_bc, ln1_w), (l1b_bc, ln1_b)):
                sp.dma_start(dst[:], src.partition_broadcast(P)).then_inc(cons_in, 16)
            sp.dma_start(xrow[:], x_by_batch[0]).then_inc(xrow_in, 16)

            def inputs(i):
                sp.wait_ge(xc_lo_ok, 2 * i)
                alone(sp)
                sp.dma_start(x_raw[:], x_t[i]).then_inc(xraw_in, 16)
                sp.dma_start(c_raw[:], ctx_t[i]).then_inc(craw_in, 16)

            def queries(i, c):
                sp.wait_ge(qk_lo_ok, NQ * i + c + 1)
                for h in range(HQ):
                    rows = slice(DK * h, DK * h + DK)
                    sp.dma_start(q_alone[rows, c % 2, :, h].bitcast(F32),
                                 qk_parts[rows, c % 2, 0:2].bitcast(F32)).then_inc(q_in[c % 2], 16)

            def hidden_weights(f):
                if f >= 2:
                    sp.wait_ge(ffw_lo_ok, f - 1)
                sp.dma_start(w_raw[:, f % 2, 0], w1[:, f].rearrange("p k m -> p (k m)")).then_inc(ffw_in[f % 2], 16)
                sp.dma_start(w_raw[:, f % 2, 1], w2[:, f]).then_inc(ffw_in[f % 2], 16)

            def rows_of(i):
                sp.wait_ge(u_ok, RT * i)
                alone(sp)
                sp.dma_start(xrow[:], x_by_batch[i]).then_inc(xrow_in, 16)

            def step(i, slot, now, last, older, ahead, load):
                if last and not now:
                    sp.wait_ge(s_mm, 16 * B)
                    hidden_weights(0)
                    hidden_weights(1)
                    sp.dma_start(x1[:, 0], x1_by_group[0]).then_inc(x1_in[0], 16)
                    sp.dma_start(b1_col[:], b1).then_inc(ffc_in, 16)
                    for dst, src in ((b2_bc, b2), (l2w_bc, ln2_w), (l2b_bc, ln2_b)):
                        sp.dma_start(dst[:], src.partition_broadcast(P)).then_inc(ffc_in, 16)
                if now:
                    queries(i, 1)
                    queries(i, 2)
                    queries(i, 3)
                if load:
                    inputs(i + 2)
                if older and last:
                    rows_of(i - 1)
                if ahead:
                    queries(i + 1, 0)
                if not last and not now:
                    for f in range(2, 6):
                        hidden_weights(f)
                if older:
                    sp.wait_ge(x1_ok, i - 1)
                    alone(sp)
                    sp.dma_start(x1_by_batch[i - 2], u_sb[:]).then_inc(x1_out, 16)

            inputs(1)
            sp.wait_ge(const_ok, CONSTS)
            queries(0, 0)
            over_batches(sp, step)

            sp.dma_start(x1[:, 1], x1_by_group[1]).then_inc(x1_in[1], 16)
            for f in range(6, FT):
                hidden_weights(f)
            sp.wait_ge(x1_out, 16 * B + 1)

            def group(g, slot, more):
                sp.wait_ge(out_ok, GT * g + GT)
                alone(sp)
                sp.dma_start(out_by_group[g], y_sb[:]).then_inc(out_st, 16)
                if more:
                    sp.dma_start(x1[:, slot], x1_by_group[g + 2]).then_inc(x1_in[slot], 16)

            with sp.Fori(0, NG // 2 - 1) as j:
                group(j * 2, 0, True)
                group(j * 2 + 1, 1, True)
            group(NG - 2, 0, False)
            for t in (1, 2, 0, 3):
                if t == 0:
                    sp.wait_ge(out_ok, GT * (NG - 1) + 1)
                else:
                    sp.wait_ge(out_last_ok, t)
                sp.dma_start(out_by_group[NG - 1, :, t], y_sb[:, t]).then_inc(out_st, 16)
            sp.wait_ge(out_st, 16 * (NG - 1 + GT))

        @block.tensor
        def _(pe):
            def turn_rows(g, slot, ks, first):
                for k in ks:
                    if k == 0:
                        pe.wait_ge(x1_in[slot], group_bytes(g, slot))
                    if first and k < 2:
                        pe.wait_ge(u_ok, RT * (B - 2) + RT)
                    else:
                        pe.wait_ge(xt_hi_ok, KT * g + k - 1)
                        pe.wait_ge(xt_lo_ok, KT * g + k - 1)
                    for t in range(GT):
                        mm = nc.tensor.transpose(xt_bank[k % 2][:, P * t:P * t + P],
                                                 x1[:, slot, t, P * k:P * k + P], ident[:])
                    mm.then_inc(xt_mm, 1)

            def hidden(g, f, first):
                if f == 0:
                    pe.wait_ge(xt_hi_ok, KT * g + KT)
                    pe.wait_ge(xt_lo_ok, KT * g + KT)
                if f >= 2 or not first:
                    pe.wait_ge(h_ok, FT * g + f - 1)
                if first:
                    pe.wait_ge(ffw_lo_ok, f + 1)
                for k in range(KT):
                    mm = three_passes(pe, h_bank[f % 2][:], ffw[:, f, 0, P * k:P * k + P], ffw[:, f, 1, P * k:P * k + P],
                                      xt_hi[:, k], xt_lo[:, k], k == 0, k == KT - 1)
                mm.then_inc(h_mm, 1)

            def project_rows(i, t, now):
                if now and t == 0:
                    pe.wait_ge(v_ok, RT * i + 2)
                elif now:
                    pe.wait_ge(qk_lo_ok, NQ * i + 4)
                else:
                    pe.wait_ge(u_ok, RT * (i - 3) + t + 1)
                    if i == B + 1 and t == 0:
                        pe.wait_ge(xt_hi_ok, KT)
                        pe.wait_ge(xt_lo_ok, KT)
                if t == 0:
                    pe.wait_ge(w_lo_ok, 2)
                    pe.wait_ge(cc_lo_ok, NQ * (i - 2) + NQ)
                rows = slice(P * t, P * t + P)
                for k in range(KT):
                    mm = three_passes(pe, pj_bank[t][:], cc_hi[:, k, rows], cc_lo[:, k, rows],
                                      wo_hi[:, k], wo_lo[:, k], k == 0, k == KT - 1)
                mm.then_inc(wo_mm, 1)

            def values(i, t):
                pe.wait_ge(qk_lo_ok, NQ * i + 2 + t)
                if isinstance(i, int) and i == 0:
                    pe.wait_ge(w_lo_ok, 1)
                rows = slice(P * t, P * t + P)
                for k in range(KT):
                    mm = three_passes(pe, pj_bank[1 - t][:], c_hi[:, k, rows], c_lo[:, k, rows],
                                      wv_hi[:, k], wv_lo[:, k], k == 0, k == KT - 1)
                mm.then_inc(v_mm, 1)

            def queries_keys(i, c, before):
                if c == 2:
                    pe.wait_ge(qk_lo_ok, NQ * i + 1)
                elif c == 3:
                    pe.wait_ge(v_ok, RT * i + 1)
                elif before:
                    pe.wait_ge(u_ok, RT * (i - 3) + c + 1)
                elif isinstance(i, int) and i > 0:
                    if c == 0:
                        pe.wait_ge(v_ok, RT * i)
                    else:
                        pe.wait_ge(qk_lo_ok, NQ * i)
                cols = slice(P * c, P * c + P)
                for n, (hi, lo) in enumerate(((x_hi, x_lo), (c_hi, c_lo))):
                    if c == 0:
                        pe.wait_ge(xc_lo_ok, 2 * i + n + 1)
                    for k in range(KT):
                        mm = three_passes(pe, pj_bank[c % 2][:, n * S:(n + 1) * S], wk_hi[:, k, cols],
                                          wk_lo[:, k, cols], hi[:, k], lo[:, k], k == 0, k == KT - 1)
                mm.then_inc(qk_mm, 1)

            def scores(i, c, heads):
                if 0 in heads:
                    pe.wait_ge(q_in[c % 2], 128 * i + 64 * (c // 2 + 1))
                for h in heads:
                    n = HQ * c + h
                    if n >= 2 or not (isinstance(i, int) and i == 0):
                        pe.wait_ge(s_ok, 16 * i + n - 1)
                    dst = s_bank[h % 2]
                    q_hi, q_lo = q_alone[:, c % 2, 0, h], q_alone[:, c % 2, 1, h]
                    k_hi, k_lo = qk_parts[:, c % 2, 2], qk_parts[:, c % 2, 3]
                    three_passes(pe, dst[:, 0:LATE], q_hi[:, P:S], q_lo[:, P:S], k_hi, k_lo, True, True)
                    three_passes(pe, dst[:, LATE:SPAN], q_hi[:, 0:P], q_lo[:, 0:P],
                                 k_hi[:, P:S], k_lo[:, P:S], True, True).then_inc(s_mm, 1)

            def transposes(i, c):
                for n in range(3 * HQ):
                    h, piece = n // 3, n % 3
                    if piece == 0:
                        pe.wait_ge(p_ok, 16 * i + HQ * c + h + 1)
                    if n % 4 == 0 and (c > 0 or not (isinstance(i, int) and i == 0)):
                        pe.wait_ge(pt_ok, 12 * i + 3 * (c - 1) + n // 4 + 1)
                    at = (LATE, P, 0)[piece]
                    mm = nc.tensor.transpose(pt_bank[n // 4][:, P * (n % 4):P * (n % 4) + P],
                                             p_sb[:, h, at:at + P], ident[:])
                    if n % 4 == 3:
                        mm.then_inc(pt_mm, 1)

            def attend_quad(i, slot, c):
                pe.wait_ge(pt_ok, 12 * i + 3 * c + 3)
                if c == 0:
                    pe.wait_ge(v_ok, RT * i + RT)
                if c > 0 or not (isinstance(i, int) and i == 0):
                    pe.wait_ge(cc_ok, NQ * i + c)
                pe.wait_ge(wide_ok, NQ * i + c + 1)
                for t in range(RT):
                    at = S + P * (1 - t)
                    nc.tensor.matmul(av_bank[:, at:at + P], zi_wide[:, t].rearrange("p h d -> p (h d)"),
                                          ident[:], start=True, stop=True, skip_group_check=True)
                for part in range(2):
                    for h in range(HQ):
                        feat = DK * (HQ * c + h)
                        rows = slice(DK * h, DK * h + DK)
                        lhs = v_sb[:, slot, 1 - part, feat:feat + DK]
                        if part == 0:
                            nc.tensor.matmul(av_bank[rows, 0:S], lhs, pt_sb[:, c % 2, h, 0:S],
                                             start=True, stop=False, skip_group_check=True)
                        else:
                            mm = nc.tensor.matmul(av_bank[rows, P:S], lhs, pt_sb[:, c % 2, h, S:SPAN],
                                             start=False, stop=True, skip_group_check=True)
                mm.then_inc(av_mm, 1)

            def step(i, slot, now, last, older, ahead, load):
                if now:
                    scores(i, 0, (2, 3))
                if older:
                    attend_quad(i - 2, slot, 3)
                if not last and not now:
                    pe.wait_ge(cc_ok, NQ * B)
                    hidden(0, 0, True)
                if now:
                    queries_keys(i, 2, older)
                if last:
                    transposes(i - 1, 0)
                if now:
                    scores(i, 1, (0, 1))
                    values(i, 0)
                    scores(i, 1, (2, 3))
                    values(i, 1)
                    queries_keys(i, 3, older)
                if last:
                    attend_quad(i - 1, 1 - slot, 0)
                if older:
                    project_rows(i, 0, now)
                if last:
                    transposes(i - 1, 1)
                if now:
                    scores(i, 2, (0, 1))
                if older:
                    project_rows(i, 1, now)
                if now:
                    scores(i, 2, (2, 3))
                if last:
                    attend_quad(i - 1, 1 - slot, 1)
                if last:
                    transposes(i - 1, 2)
                if now:
                    scores(i, 3, (0, 1))
                if ahead:
                    queries_keys(i + 1, 0, older)
                if now:
                    scores(i, 3, (2, 3))
                if last:
                    attend_quad(i - 1, 1 - slot, 2)
                    transposes(i - 1, 3)
                if ahead:
                    queries_keys(i + 1, 1, older)
                if ahead:
                    scores(i + 1, 0, (0, 1))
                if last and not now:
                    turn_rows(0, 0, range(KT), True)

            pe.wait_ge(wk_lo_ok, 1)
            pe.wait_ge(const_ok, CONSTS)
            queries_keys(0, 0, False)
            queries_keys(0, 1, False)
            scores(0, 0, (0, 1))
            over_batches(pe, step)

            def add_hidden(g, f, first):
                pe.wait_ge(h_hi_ok, FT * g + f + 1)
                pe.wait_ge(h_lo_ok, FT * g + f + 1)
                for t in range(GT):
                    if f == 0 and not first:
                        pe.wait_ge(y_ok, GT * (g - 1) + t + 1)
                    rows = slice(P * t, P * t + P)
                    mm = three_passes(pe, y_bank[t][:], h_hi[:, f % 2, rows], h_lo[:, f % 2, rows],
                                      ffw[:, f, 2], ffw[:, f, 3], f == 0, f == FT - 1)
                mm.then_inc(y_step, 1)

            def group(g, slot, first, last):
                for f in range(FT):
                    if not (first and f == 0):
                        hidden(g, f, first)
                    if f == FT - 1 and not last:
                        turn_rows(g + 1, 1 - slot, (0, 1), False)
                    if f >= 1:
                        add_hidden(g, f - 1, first)
                if not last:
                    turn_rows(g + 1, 1 - slot, (2, 3), False)
                add_hidden(g, FT - 1, first)

            over_groups(pe, group)

        @block.scalar
        def _(act):
            act.wait_ge(gam_dve, 1)
            nc.scalar.activation(g_tmp[:, 1], g_tmp[:, 0], ACT.Exp).then_inc(gam_act, 1)
            act.wait_ge(const_ok, CONSTS)
            act.wait_ge(col_in, 32)

            def rows_high(g, first):
                for k in range(KT):
                    act.wait_ge(xt_mm, KT * g + k + 1)
                    if k == 0 and not first:
                        act.wait_ge(h_mm, FT * g)
                    nc.scalar.copy(xt_hi[:, k], xt_bank[k % 2][:]).then_inc(xt_hi_ok, 1)

            def qk_high(i, c):
                act.wait_ge(qk_mm, NQ * i + c + 1)
                if c >= 2:
                    act.wait_ge(s_mm, 16 * i + HQ * (c - 1))
                elif not (isinstance(i, int) and i == 0):
                    act.wait_ge(s_mm, 16 * (i - 1) + HQ * (c + 3))
                nc.scalar.activation(qk_parts[:, c % 2, 0:4:2], pj_bank[c % 2][:].rearrange("p (n s) -> p n s", n=2),
                                     ACT.Identity, bias=bk_col[:, c:c + 1]).then_inc(qk_hi_ok, 1)

            def first_exp(i, c, last):
                act.wait_ge(nm1_ok, NQ * i + c + 1)
                if last:
                    act.wait_ge(p_ok, 16 * (i - 1) + HQ * c + HQ)
                for h in range(HQ):
                    a, z = head_block(c, h, True)
                    nc.scalar.activation(w_sb[:, c, a + 1:z + 1], s_sb[:, c, h, 0:LATE], ACT.Exp, scale=SCALE,
                                         bias=nm1[:, c, h, 0:1])
                act.wait_ge(shifted_ok, NQ * i + c + 1)
                early = w_sb[:, c].rearrange("p (h w) -> p h w", h=HQ)[:, :, LATE + 2:BLK]
                nc.scalar.activation(early, early, ACT.Exp, scale=SCALE).then_inc(e1_ok, 1)

            def roots(i, c):
                act.wait_ge(r_ok, NQ * i + c + 2)
                nc.scalar.activation(w_sb[:, c:c + 2], w_sb[:, c:c + 2], ACT.Sqrt, bias=tiny[:]).then_inc(root_ok, 2)

            def effect(i, c):
                act.wait_ge(root_ok, NQ * i + c + 1)
                nc.scalar.activation(w_sb[:, c], w_sb[:, c], ACT.Exp, scale=-1.0).then_inc(te_ok, 1)

            def second_exp(i, c):
                act.wait_ge(nm2_ok, NQ * i + c + 1)
                for h in range(HQ):
                    if c >= 1 or not (isinstance(i, int) and i == 0):
                        act.wait_ge(pt_mm, 12 * i + 3 * (c - 1) + (1, 2, 3, 3)[h])
                    for late in (True, False):
                        a, z = head_block(c, h, late)
                        dst = p_sb[:, h, 0:LATE] if late else p_sb[:, h, LATE:SPAN]
                        t = 0 if late else 1
                        e = nc.scalar.activation(dst, w_sb[:, c, a:z], ACT.Exp, scale=SCALE,
                                                 bias=nm2[:, c, h, t:t + 1], accum_out=z2[:, c, h, t:t + 1])
                    e.then_inc(p_ok, 1)

            def turned(i, c):
                flat = pt_sb[:, c % 2].rearrange("p h s -> p (h s)")
                for n in range(3):
                    act.wait_ge(pt_mm, 12 * i + 3 * c + n + 1)
                    if n == 0 and (c >= 2 or not (isinstance(i, int) and i == 0)):
                        act.wait_ge(av_mm, NQ * i + c - 1)
                    nc.scalar.copy(flat[:, 512 * n:512 * n + 512], pt_bank[n][:]).then_inc(pt_ok, 1)

            def reciprocals(i, c):
                act.wait_ge(av_mm, NQ * i + c + 1)
                if c >= 2 or not (isinstance(i, int) and i == 0):
                    act.wait_ge(cc_lo_ok, NQ * i + c - 1)
                nc.scalar.copy(cc_sb[:, c % 2], av_bank[:, S:2 * S]).then_inc(zi_row_ok, 1)

            def step(i, slot, now, last, older, ahead, load):
                for c in range(NQ):
                    if last:
                        second_exp(i - 1, c)
                    if c == 3 and ahead:
                        qk_high(i + 1, 0)
                    if c == 0 and older:
                        reciprocals(i - 2, 3)
                    if c == 1 and last:
                        roots(i - 1, 2)
                    if c == 1 and last:
                        effect(i - 1, 2)
                        effect(i - 1, 3)
                    if c == 1 and now:
                        qk_high(i, 3)
                    if c == 3 and now:
                        roots(i, 0)
                        effect(i, 0)
                        effect(i, 1)
                    if c > 0 and last:
                        reciprocals(i - 1, c - 1)
                    if c == 3 and ahead:
                        qk_high(i + 1, 1)
                    if now:
                        first_exp(i, c, last)
                    if c == 0 and now:
                        qk_high(i, 2)
                    if last:
                        turned(i - 1, c)
                if last and not now:
                    rows_high(0, True)

            qk_high(0, 0)
            qk_high(0, 1)
            over_batches(act, step)

            act.wait_ge(ffc_in, 16 * 4)

            def group(g, slot, first, last):
                for f in range(FT):
                    act.wait_ge(h_mm, FT * g + f + 1)
                    if f >= 2 or not first:
                        act.wait_ge(h_lo_ok, FT * g + f - 1)
                    nc.scalar.activation(h_sb[:, f % 2], h_bank[f % 2][:], ACT.Relu,
                                         bias=b1_col[:, f:f + 1]).then_inc(h_ok, 1)
                    act.wait_ge(h_ok, FT * g + f + 1)
                    if f >= 2 or not first:
                        act.wait_ge(y_step, FT * g + f - 1)
                    nc.scalar.copy(h_hi[:, f % 2], h_sb[:, f % 2]).then_inc(h_hi_ok, 1)
                if not last:
                    rows_high(g + 1, False)

            over_groups(act, group)

        @block.vector
        def _(dve):
            def weight_high(n, hi):
                dve.wait_ge(wraw_in[n], 16)
                nc.vector.tensor_copy(hi[:].rearrange("p k n -> p (k n)"),
                                      s_sb_flat(s_sb)[:, n * KT * D:(n + 1) * KT * D]).then_inc(w_hi_ok, 1)

            weight_high(0, wk_hi)
            dve.wait_ge(w_hi_ok, 1)
            nc.vector.tensor_tensor(wk_lo[:].rearrange("p k n -> p (k n)"), s_sb_flat(s_sb)[:, 0:KT * D],
                                    wk_hi[:].rearrange("p k n -> p (k n)").bitcast(F32),
                                    ALU.subtract).then_inc(wk_lo_ok, 1)

            def split_inputs(i, done):
                dve.wait_ge(xraw_in, 16 * i + 16)
                dve.wait_ge(craw_in, 16 * i + 16)
                if done:
                    dve.wait_ge(qk_mm, NQ * i)
                    dve.wait_ge(v_mm, RT * i)
                nc.vector.tensor_copy(x_hi[:], x_raw[:]).then_inc(xc_hi_ok, 1)
                nc.vector.tensor_copy(c_hi[:], c_raw[:]).then_inc(xc_hi_ok, 1)

            split_inputs(0, False)
            weight_high(1, wv_hi)
            weight_high(2, wo_hi)
            dve.wait_ge(col_in, 32)
            chain = [0]

            def then(ins):
                chain[0] += 1
                ins.then_inc(gam_dve, 1)
                dve.wait_ge(gam_dve, chain[0])

            minus_abs, y, two_y, inv, z, zz, acc, sp = (g_tmp[:, n] for n in range(8))
            then(nc.vector.scalar_tensor_tensor(minus_abs, g_in[:], -1.0, g_in[:], ALU.mult, ALU.min))
            dve.wait_ge(gam_act, 1)
            then(nc.vector.tensor_scalar(two_y, y, 2.0, None, ALU.add))
            then(nc.vector.reciprocal(inv, two_y))
            then(nc.vector.tensor_tensor(z, y, inv, ALU.mult))
            then(nc.vector.tensor_tensor(zz, z, z, ALU.mult))
            then(nc.vector.tensor_scalar(acc, zz, 1.0 / 15, None, ALU.mult))
            for n in range(13, 1, -2):
                then(nc.vector.scalar_tensor_tensor(acc, acc, 1.0 / n, zz, ALU.add, ALU.mult))
            then(nc.vector.scalar_tensor_tensor(acc, acc, 1.0, z, ALU.add, ALU.mult))
            then(nc.vector.tensor_scalar(acc, acc, 2.0, None, ALU.mult))
            then(nc.vector.scalar_tensor_tensor(sp, g_in[:], 0.0, acc, ALU.max, ALU.add))
            for t in range(2):
                then(nc.vector.tensor_tensor(gamma2[:, :, t], sp, sp, ALU.mult))
            dve.wait_ge(const_ok, CONSTS)
            dve.wait_ge(wk_lo_ok, 1)

            def weights_high(f):
                dve.wait_ge(ffw_in[f % 2], 32 * (f // 2 + 1))
                nc.vector.tensor_copy(ffw[:, f, 0:4:2], w_raw[:, f % 2]).then_inc(ffw_hi_ok, 1)

            def rows_low(g):
                for k in range(KT):
                    dve.wait_ge(xt_hi_ok, KT * g + k + 1)
                    nc.vector.tensor_tensor(xt_lo[:, k], xt_bank[k % 2][:], xt_hi[:, k].bitcast(F32),
                                            ALU.subtract).then_inc(xt_lo_ok, 1)

            def qk_low(i, c):
                dve.wait_ge(qk_hi_ok, NQ * i + c + 1)
                src = pj_bank[c % 2][:].rearrange("p (n s) -> p n s", n=2)
                nc.vector.scalar_tensor_tensor(qk_parts[:, c % 2, 1:4:2], src, bk_col[:, c:c + 1],
                                               qk_parts[:, c % 2, 0:4:2].bitcast(F32), ALU.add,
                                               ALU.subtract).then_inc(qk_lo_ok, 1)

            def value_rows(i, slot, t, older):
                if isinstance(i, int) and i == 0:
                    dve.wait_ge(cons_in, 16 * 4)
                if older and t == 0:
                    dve.wait_ge(av_mm, NQ * (i - 2) + NQ)
                dve.wait_ge(v_mm, RT * i + t + 1)
                nc.vector.tensor_tensor(v_sb[:, slot, t], pj_bank[1 - t][:], bv_bc[:], ALU.add).then_inc(v_ok, 1)

            def mask_scores(i, c, heads):
                for h in heads:
                    dve.wait_ge(s_mm, 16 * i + HQ * c + h + 1)
                    alone(dve)
                    nc.vector.tensor_tensor_reduce(
                        out=s_sb[:, c, h, 0:LATE], in0=s_bank[h % 2][:, 0:LATE], in1=mask[:],
                        scale=1.0, scalar=NEG, op0=ALU.add, op1=ALU.max, accum_out=m1[:, c, h, 0:1])
                    nc.vector.tensor_tensor_reduce(
                        out=s_sb[:, c, h, LATE:SPAN], in0=s_bank[h % 2][:, LATE:SPAN], in1=mask[:, 0:EARLY],
                        scale=1.0, scalar=NEG, op0=ALU.add, op1=ALU.max,
                        accum_out=m1[:, c, h, 1:2]).then_inc(s_ok, 1)
                if HQ - 1 in heads:
                    dve.wait_ge(s_ok, 16 * i + HQ * c + HQ)
                    nc.vector.tensor_scalar(nm1[:, c], m1[:, c], -SCALE, None, ALU.mult).then_inc(nm1_ok, 1)

            def running_sums(i, c):
                dve.wait_ge(e1_ok, NQ * i + c + 1)
                blocks = w_sb[:, c].rearrange("p (h w) -> p h w", h=HQ)
                dve.wait_ge(zero_ok, NQ * i + c + 1)
                nc.vector.tensor_tensor_scan(w_sb[:, c], carry[:], w_sb[:, c], 0.0,
                                             ALU.mult, ALU.add).then_inc(scan_ok, 1)
                dve.wait_ge(scan_ok, NQ * i + c + 1)
                nc.vector.reciprocal(zi[:, c], blocks[:, :, LATE:BLK:EARLY + 1]).then_inc(zi_ok, 1)
                dve.wait_ge(zi_ok, NQ * i + c + 1)
                nc.vector.tensor_tensor(gz[:, c], zi[:, c], gamma2[:, HQ * c:HQ * c + HQ],
                                        ALU.mult).then_inc(gz_ok, 1)

            def decay(i, c):
                dve.wait_ge(t_ok, NQ * i + c + 1)
                dve.wait_ge(gz_ok, NQ * i + c + 1)
                for h in range(HQ):
                    for t in range(2):
                        a, z = head_block(c, h, t == 0)
                        r = nc.vector.tensor_scalar(w_sb[:, c, a:z], w_sb[:, c, a:z], gz[:, c, h, t:t + 1],
                                                    R_MAX, ALU.mult, ALU.min)
                r.then_inc(r_ok, 1)

            def decayed_scores(i, c):
                dve.wait_ge(te_ok, NQ * i + c + 1)
                alone(dve)
                for h in range(HQ):
                    for t in range(2):
                        a, z = head_block(c, h, t == 0)
                        src = s_sb[:, c, h, 0:LATE] if t == 0 else s_sb[:, c, h, LATE:SPAN]
                        r = nc.vector.tensor_tensor_reduce(
                            out=w_sb[:, c, a:z], in0=w_sb[:, c, a:z], in1=src, scale=1.0, scalar=NEG,
                            op0=ALU.mult, op1=ALU.max, accum_out=m2[:, c, h, t:t + 1])
                r.then_inc(s2_ok, 1)
                dve.wait_ge(s2_ok, NQ * i + c + 1)
                nc.vector.tensor_scalar(nm2[:, c], m2[:, c], -SCALE, None, ALU.mult).then_inc(nm2_ok, 1)

            def totals(i, c):
                dve.wait_ge(p_ok, 16 * i + HQ * c + HQ)
                nc.vector.reciprocal(z2[:, c], z2[:, c]).then_inc(zi2_ok, 1)
                dve.wait_ge(zi2_ok, NQ * i + c + 1)
                if c > 0 or not (isinstance(i, int) and i == 0):
                    dve.wait_ge(av_mm, NQ * i + c)
                nc.vector.tensor_copy(zi_wide[:].rearrange("p t h d -> p h t d"),
                                      z2[:, c].unsqueeze(3).broadcast_to([P, HQ, 2, DK])).then_inc(wide_ok, 1)

            def concat(i, c):
                dve.wait_ge(zi_row_ok, NQ * i + c + 1)
                nc.vector.tensor_tensor(cc_sb[:, c % 2], av_bank[:, 0:S], cc_sb[:, c % 2], ALU.mult).then_inc(cc_ok, 1)

            def residual(i, t):
                dve.wait_ge(xb_ok, i + 1)
                if t == 0 and not (isinstance(i, int) and i == 0):
                    dve.wait_ge(x1_out, 16 * i + 1)
                dve.wait_ge(wo_mm, RT * i + t + 1)
                nc.vector.tensor_tensor(u_sb[:, t], pj_bank[t][:], xrow[:, t], ALU.add).then_inc(u_ok, 1)

            def moments(i):
                for t in range(RT):
                    dve.wait_ge(u_ok, RT * i + t + 1)
                    nc.vector.bn_stats(bn1[:, t], u_sb[:, t]).then_inc(bn1_ok, 1)
                for t in range(RT):
                    dve.wait_ge(bn1_ok, RT * i + t + 1)
                    alone(dve)
                    nc.vector.bn_aggr(mv1[:, t], bn1[:, t]).then_inc(mv1_ok, 1)

            def normalise(i):
                dve.wait_ge(rstd1_ok, i + 1)
                for t in range(RT):
                    nc.vector.tensor_scalar(u_sb[:, t], u_sb[:, t], mv1[:, t, 0:1], rstd1[:, t:t + 1],
                                            ALU.subtract, ALU.mult).then_inc(norm1_ok, 1)

            def step(i, slot, now, last, older, ahead, load):
                if now:
                    mask_scores(i, 0, (0, 1))
                if older:
                    concat(i - 2, 2)
                if last:
                    decay(i - 1, 2)
                if now:
                    mask_scores(i, 0, (2, 3))
                    qk_low(i, 1)
                if last:
                    running_sums(i - 1, 3)
                    decayed_scores(i - 1, 1)
                if now:
                    qk_low(i, 2)
                if older:
                    concat(i - 2, 3)
                if not last and not now:
                    dve.wait_ge(p_ok, 16 * B)
                    weights_high(2)
                    weights_high(3)
                if last:
                    decay(i - 1, 3)
                    totals(i - 1, 0)
                if now:
                    if not last:
                        dve.wait_ge(w_lo_ok, 2)
                    mask_scores(i, 1, (0, 1))
                    value_rows(i, slot, 0, older)
                    mask_scores(i, 1, (2, 3))
                    running_sums(i, 0)
                    value_rows(i, slot, 1, older)
                if last and not now:
                    weights_high(0)
                    weights_high(1)
                if ahead:
                    split_inputs(i + 1, True)
                if now:
                    decay(i, 0)
                if last:
                    decayed_scores(i - 1, 2)
                if older:
                    residual(i - 2, 0)
                if now:
                    qk_low(i, 3)
                    mask_scores(i, 2, (0, 1))
                if last:
                    concat(i - 1, 0)
                if last:
                    totals(i - 1, 1)
                if older:
                    residual(i - 2, 1)
                if now:
                    mask_scores(i, 2, (2, 3))
                    running_sums(i, 1)
                if last:
                    decayed_scores(i - 1, 3)
                if now:
                    mask_scores(i, 3, (0, 1))
                if last:
                    concat(i - 1, 1)
                if now:
                    decay(i, 1)
                if last:
                    totals(i - 1, 2)
                if now:
                    mask_scores(i, 3, (2, 3))
                if older:
                    moments(i - 2)
                if ahead:
                    qk_low(i + 1, 0)
                if now:
                    running_sums(i, 2)
                if older:
                    normalise(i - 2)
                if last:
                    totals(i - 1, 3)
                if last and not now:
                    rows_low(0)
                if now:
                    decayed_scores(i, 0)

            qk_low(0, 0)
            over_batches(dve, step)

            def group_moments(g):
                for t in range(GT):
                    dve.wait_ge(y_ok, GT * g + t + 1)
                    nc.vector.bn_stats(bn2[:, t], y_sb[:, t]).then_inc(bn2_ok, 1)
                for t in range(GT):
                    dve.wait_ge(bn2_ok, GT * g + t + 1)
                    alone(dve)
                    nc.vector.bn_aggr(mv2[:, t], bn2[:, t]).then_inc(mv2_ok, 1)

            def group_normalise(g):
                dve.wait_ge(rstd2_ok, g + 1)
                for t in range(GT):
                    nc.vector.tensor_scalar(y_sb[:, t], y_sb[:, t], mv2[:, t, 0:1], rstd2[:, t:t + 1],
                                            ALU.subtract, ALU.mult).then_inc(norm2_ok, 1)

            def group(g, slot, first, last):
                for f in range(FT):
                    dve.wait_ge(h_hi_ok, FT * g + f + 1)
                    nc.vector.tensor_tensor(h_lo[:, f % 2], h_sb[:, f % 2], h_hi[:, f % 2].bitcast(F32),
                                            ALU.subtract).then_inc(h_lo_ok, 1)
                    if first and f + 4 < FT:
                        if f + 4 == EARLY_TILES:
                            dve.wait_ge(x1_out, 16 * B + 1)
                        weights_high(f + 4)
                    if f == 1 and not first:
                        group_moments(g - 1)
                    if f == 3 and not first:
                        group_normalise(g - 1)
                if not last:
                    rows_low(g + 1)
                dve.wait_ge(y_step, FT * g + FT)
                dve.wait_ge(xb2_ok, g + 1)
                if not first:
                    dve.wait_ge(out_st, 16 * g)
                for t in range(GT):
                    nc.vector.tensor_tensor(y_sb[:, t], y_bank[t][:], x1[:, slot, t], ALU.add).then_inc(y_ok, 1)
                if last:
                    group_moments(g)
                    dve.wait_ge(rstd2_ok, NG)
                    nc.vector.tensor_scalar(y_sb[:, 0], y_sb[:, 0], mv2[:, 0, 0:1], rstd2[:, 0:1],
                                            ALU.subtract, ALU.mult).then_inc(norm2_ok, 1)
                    for t in range(1, GT):
                        nc.vector.scalar_tensor_tensor(y_sb[:, t], y_sb[:, t], mv2[:, t, 0:1], l2w_bc[:],
                                                       ALU.subtract, ALU.mult).then_inc(scaled_last_ok, 1)
                        dve.wait_ge(scaled_last_ok, t)
                        nc.vector.scalar_tensor_tensor(y_sb[:, t], y_sb[:, t], rstd2[:, t:t + 1], l2b_bc[:],
                                                       ALU.mult, ALU.add).then_inc(out_last_ok, 1)

            over_groups(dve, group)

        @block.gpsimd
        def _(pool):
            nc.gpsimd.iota(iota_i, pattern=[[1, S]], base=1 - P, channel_multiplier=1).then_inc(const_ok, 1)
            nc.gpsimd.memset(mask[:], 0.0).then_inc(const_ok, 1)
            nc.gpsimd.memset(ident[:], 0.0).then_inc(const_ok, 1)
            nc.gpsimd.memset(carry[:], 1.0).then_inc(const_ok, 1)
            nc.gpsimd.memset(half[:], -0.5).then_inc(const_ok, 1)
            nc.gpsimd.memset(tiny[:], R_TINY).then_inc(const_ok, 1)
            nc.gpsimd.memset(q_alone[:].bitcast(F32), 0.0).then_inc(const_ok, 1)
            pool.wait_ge(const_ok, 7)
            nc.gpsimd.tensor_copy(dist[:], iota_i).then_inc(const_ok, 1)
            nc.gpsimd.affine_select(out=mask[:], in_=mask[:], compare_op=ALU.is_ge, fill=NEG, base=1 - P,
                                    pattern=[[1, S]], channel_multiplier=1).then_inc(const_ok, 1)
            nc.gpsimd.affine_select(out=ident[:], in_=ident[:], compare_op=ALU.not_equal, fill=1.0, base=0,
                                    pattern=[[-1, P]], channel_multiplier=1).then_inc(const_ok, 1)
            nc.gpsimd.memset(carry[:].rearrange("p (h w) -> p h w", h=HQ)[:, :, 0:LATE + 2:LATE + 1],
                             0.0).then_inc(const_ok, 1)
            def split_inputs(i):
                for n, (raw, hi, lo) in enumerate(((x_raw, x_hi, x_lo), (c_raw, c_hi, c_lo))):
                    pool.wait_ge(xc_hi_ok, 2 * i + n + 1)
                    nc.gpsimd.tensor_tensor(lo[:], raw[:], hi[:].bitcast(F32), ALU.subtract).then_inc(xc_lo_ok, 1)

            split_inputs(0)
            for n, (hi, lo) in enumerate(((wv_hi, wv_lo), (wo_hi, wo_lo))):
                pool.wait_ge(w_hi_ok, n + 2)
                nc.gpsimd.tensor_tensor(lo[:].rearrange("p k n -> p (k n)"),
                                        s_sb_flat(s_sb)[:, (n + 1) * KT * D:(n + 2) * KT * D],
                                        hi[:].rearrange("p k n -> p (k n)").bitcast(F32),
                                        ALU.subtract).then_inc(w_lo_ok, 1)
            pool.wait_ge(const_ok, CONSTS)
            pool.wait_ge(cons_in, 16 * 4)

            def weights_low(f):
                pool.wait_ge(ffw_hi_ok, f + 1)
                nc.gpsimd.tensor_tensor(ffw[:, f, 1:4:2], w_raw[:, f % 2], ffw[:, f, 0:4:2].bitcast(F32),
                                        ALU.subtract).then_inc(ffw_lo_ok, 1)

            def add_bias(i):
                pool.wait_ge(xrow_in, 16 * i + 16)
                nc.gpsimd.tensor_tensor(xrow[:], xrow[:], bo_bc[:].unsqueeze(1).broadcast_to([P, RT, D]),
                                        ALU.add).then_inc(xb_ok, 1)

            def times_distance(i, c):
                pool.wait_ge(scan_ok, NQ * i + c + 1)
                blocks = w_sb[:, c].rearrange("p (h w) -> p h w", h=HQ)
                nc.gpsimd.tensor_tensor(blocks[:, :, 0:LATE], blocks[:, :, 0:LATE],
                                        dist[:].unsqueeze(1).broadcast_to([P, HQ, LATE]), ALU.mult)
                nc.gpsimd.tensor_tensor(blocks[:, :, LATE + 1:BLK - 1], blocks[:, :, LATE + 1:BLK - 1],
                                        dist[:, 0:EARLY].unsqueeze(1).broadcast_to([P, HQ, EARLY]),
                                        ALU.mult).then_inc(t_ok, 1)

            def shift_early(i, c, last):
                pool.wait_ge(nm1_ok, NQ * i + c + 1)
                if last:
                    pool.wait_ge(p_ok, 16 * (i - 1) + HQ * c + HQ)
                alone(pool)
                blocks = w_sb[:, c].rearrange("p (h w) -> p h w", h=HQ)
                nc.gpsimd.memset(blocks[:, :, 0:LATE + 2:LATE + 1], 0.0).then_inc(zero_ok, 1)
                nc.gpsimd.tensor_tensor(blocks[:, :, LATE + 2:BLK], s_sb[:, c, :, LATE:SPAN],
                                        m1[:, c, :, 1:2].broadcast_to([P, HQ, EARLY]),
                                        ALU.subtract).then_inc(shifted_ok, 1)

            def split_concat(i, c):
                pool.wait_ge(cc_ok, NQ * i + c + 1)
                if c == 0 and not (isinstance(i, int) and i == 0):
                    pool.wait_ge(wo_mm, RT * i)
                alone(pool)
                nc.gpsimd.tensor_copy(cc_hi[:, c], cc_sb[:, c % 2]).then_inc(cc_hi_ok, 1)
                pool.wait_ge(cc_hi_ok, NQ * i + c + 1)
                nc.gpsimd.tensor_tensor(cc_lo[:, c], cc_sb[:, c % 2], cc_hi[:, c].bitcast(F32),
                                        ALU.subtract).then_inc(cc_lo_ok, 1)

            def deviation(i):
                pool.wait_ge(mv1_ok, RT * i + RT)
                alone(pool)
                nc.gpsimd.tensor_scalar(rstd1[:], mv1[:, :, 1], EPS_LN, None, ALU.add).then_inc(ve1_ok, 1)
                pool.wait_ge(ve1_ok, i + 1)
                nc.gpsimd.tensor_tensor(rstd1[:], rstd1[:], half[:, 0:RT], ALU.pow).then_inc(rstd1_ok, 1)

            def scale_shift(i):
                pool.wait_ge(norm1_ok, RT * i + RT)
                nc.gpsimd.tensor_tensor(u_sb[:], u_sb[:], l1w_bc[:].unsqueeze(1).broadcast_to([P, RT, D]),
                                        ALU.mult).then_inc(scaled1_ok, 1)
                pool.wait_ge(scaled1_ok, i + 1)
                nc.gpsimd.tensor_tensor(u_sb[:], u_sb[:], l1b_bc[:].unsqueeze(1).broadcast_to([P, RT, D]),
                                        ALU.add).then_inc(x1_ok, 1)

            def step(i, slot, now, last, older, ahead, load):
                if now:
                    shift_early(i, 0, last)
                if last:
                    times_distance(i - 1, 3)
                if older:
                    split_concat(i - 2, 2)
                    split_concat(i - 2, 3)
                    add_bias(i - 2)
                if last and not now:
                    weights_low(0)
                    weights_low(1)
                if not last and not now:
                    weights_low(2)
                    weights_low(3)
                if now:
                    shift_early(i, 1, last)
                    times_distance(i, 0)
                if ahead:
                    split_inputs(i + 1)
                if last:
                    split_concat(i - 1, 0)
                if now:
                    shift_early(i, 2, last)
                    times_distance(i, 1)
                if last:
                    split_concat(i - 1, 1)
                if now:
                    shift_early(i, 3, last)
                if older:
                    deviation(i - 2)
                if now:
                    times_distance(i, 2)
                if older:
                    scale_shift(i - 2)

            over_batches(pool, step)

            pool.wait_ge(ffc_in, 16 * 4)

            def group_norm(g, tiles):
                pool.wait_ge(mv2_ok, GT * g + GT)
                alone(pool)
                nc.gpsimd.tensor_scalar(rstd2[:], mv2[:, :, 1], EPS_LN, None, ALU.add).then_inc(ve2_ok, 1)
                pool.wait_ge(ve2_ok, g + 1)
                nc.gpsimd.tensor_tensor(rstd2[:], rstd2[:], half[:], ALU.pow).then_inc(rstd2_ok, 1)
                for t in range(tiles):
                    pool.wait_ge(norm2_ok, GT * g + t + 1)
                    nc.gpsimd.tensor_tensor(y_sb[:, t], y_sb[:, t], l2w_bc[:], ALU.mult).then_inc(scaled2_ok, 1)
                    pool.wait_ge(scaled2_ok, GT * g + t + 1)
                    nc.gpsimd.tensor_tensor(y_sb[:, t], y_sb[:, t], l2b_bc[:], ALU.add).then_inc(out_ok, 1)

            def group(g, slot, first, last):
                if first:
                    for f in range(4, FT):
                        weights_low(f)
                else:
                    group_norm(g - 1, GT)
                pool.wait_ge(xt_mm, KT * g + KT)
                nc.gpsimd.tensor_tensor(x1[:, slot], x1[:, slot], b2_bc[:].unsqueeze(1).broadcast_to([P, GT, D]),
                                        ALU.add).then_inc(xb2_ok, 1)
                if last:
                    group_norm(g, 1)

            over_groups(pool, group)


CONSTS = 11


def s_sb_flat(s_sb):
    return s_sb[:].rearrange("p c h w -> p (c h w)")


def group_bytes(g, slot):
    return 16 * (g // 2 + 1) if isinstance(g, int) else 8 * (g - slot) + 16


def kernel(**inputs):
    import numpy as np
    import concourse.bacc as bacc
    from concourse.bass_utils import run_bass_kernel_spmd

    a = {k.removeprefix("L0_xattn_"): np.asarray(v) for k, v in inputs.items()}
    x, ctx = a["x"], a["ctx_1024"]
    B, S, D = x.shape
    F = a["b1"].shape[0]
    kt, ft = D // P, F // P

    def features_first(t):
        return t.reshape(B, S, kt, P).transpose(0, 3, 2, 1)

    def weight(w):
        return w.reshape(w.shape[0], w.shape[1] // P, P).transpose(2, 1, 0)

    arrays = {
        "x_rows": x, "x_t": features_first(x), "ctx_t": features_first(ctx[:, ::-1]),
        "wk": weight(a["Wk"]), "bk": a["bk"].reshape(kt, P).transpose(1, 0),
        "wv": weight(a["Wv"]), "bv": a["bv"], "wo": weight(a["Wo"]), "bo": a["bo"],
        "gammas": a["gammas"].reshape(-1), "ln1_w": a["ln1_w"], "ln1_b": a["ln1_b"],
        "w1": a["W1"].reshape(ft, P, kt, P).transpose(3, 0, 2, 1), "b1": a["b1"].reshape(ft, P).transpose(1, 0),
        "w2": weight(a["W2"]), "b2": a["b2"], "ln2_w": a["ln2_w"], "ln2_b": a["ln2_b"],
    }
    arrays = {k: np.ascontiguousarray(v) for k, v in arrays.items()}
    nc = bacc.Bacc("TRN2", target_bir_lowering=False, num_devices=1)
    aps = [nc.dram_tensor(k, v.shape, mybir.dt.from_np(v.dtype), kind="ExternalInput").ap()
           for k, v in arrays.items()]
    out = nc.dram_tensor("out", (B, S, D), F32, kind="ExternalOutput").ap()
    build(nc, *aps, out)
    r = run_bass_kernel_spmd(nc, [arrays], core_ids=[0])
    return r.results[0]["out"]
```
